# Optimizing a Trainium2 kernel written in Bass

```python
import numpy as np
import jax
import jax.numpy as jnp

def _softmax(x, axis=-1):
    return jax.nn.softmax(x, axis=axis)

def _gelu(x):
    return jax.nn.gelu(x, approximate=True)

def _silu(x):
    return jax.nn.silu(x)

def _sigmoid(x):
    return jax.nn.sigmoid(x)

def _layernorm(x, axis=-1, eps=1e-05):
    m = jnp.mean(x, axis=axis, keepdims=True)
    v = jnp.var(x, axis=axis, keepdims=True)
    return (x - m) / jnp.sqrt(v + eps)

def _scatter_add(tgt, idx, src, axis=0):
    return tgt.at[idx].add(src)

def _segment_sum(src, seg, n):
    return jax.ops.segment_sum(src, seg, n)
kernel_name = 'mk_seq_preln_d1_jaxref_r2_8c6c0f'

def setup_inputs(seed: int=0):
    np.random.seed(seed)
    _w = jnp.asarray

    def _L0_attn_setup():
        import math
        import jax, jax.numpy as jnp
        import numpy as np
        D_MODEL = 512
        NHEAD = 16
        DK = D_MODEL // NHEAD
        FACTOR = 5
        B, L = (4, 4096)
        U = max(1, min(FACTOR * math.ceil(math.log(L + 1)), L))
        key = jax.random.key(seed)
        ks = jax.random.split(key, 10)
        s = 1.0 / math.sqrt(D_MODEL)
        inp = {'x': jax.random.normal(ks[0], (B, L, D_MODEL), dtype=jnp.float32), 'Wq': jax.random.normal(ks[1], (D_MODEL, D_MODEL), dtype=jnp.float32) * s, 'bq': jnp.zeros((D_MODEL,), dtype=jnp.float32), 'Wk': jax.random.normal(ks[2], (D_MODEL, D_MODEL), dtype=jnp.float32) * s, 'bk': jnp.zeros((D_MODEL,), dtype=jnp.float32), 'Wv': jax.random.normal(ks[3], (D_MODEL, D_MODEL), dtype=jnp.float32) * s, 'bv': jnp.zeros((D_MODEL,), dtype=jnp.float32), 'Wo': jax.random.normal(ks[4], (D_MODEL, D_MODEL), dtype=jnp.float32) * s, 'bo': jnp.zeros((D_MODEL,), dtype=jnp.float32), 'idx_k': jax.random.permutation(ks[5], L)[:U].astype(jnp.int32)}
        return inp
    _L0_attn_in = _L0_attn_setup()

    def _L0_ffn_setup():
        import jax, jax.numpy as jnp
        import numpy as np
        B, N, D = (4, 1024, 512)
        SPARSITY = 0.01
        key = jax.random.key(seed)
        k1, k2, k3 = jax.random.split(key, 3)
        x = jax.random.normal(k1, (B, N, D), dtype=jnp.float32)
        spatial = jax.random.normal(k2, (D, D), dtype=jnp.float32) * 0.02
        freq = jnp.fft.fft(spatial, axis=-1)
        k = int(D * SPARSITY)
        mag = jnp.abs(freq)
        kth = jax.lax.top_k(mag, k)[0][:, -1:]
        w_sparse = jnp.where(mag >= kth, freq, 0.0 + 0j)
        bias = jax.random.normal(k3, (D,), dtype=jnp.float32) * 0.01
        return {'x': x, 'w_freq_real': jnp.real(w_sparse).astype(jnp.float32), 'w_freq_imag': jnp.imag(w_sparse).astype(jnp.float32), 'bias': bias}
    _L0_ffn_in = _L0_ffn_setup()
    _d = {'L0_attn_x': _L0_attn_in['x'], 'L0_attn_Wq': _L0_attn_in['Wq'], 'L0_attn_bq': _L0_attn_in['bq'], 'L0_attn_Wk': _L0_attn_in['Wk'], 'L0_attn_bk': _L0_attn_in['bk'], 'L0_attn_Wv': _L0_attn_in['Wv'], 'L0_attn_bv': _L0_attn_in['bv'], 'L0_attn_Wo': _L0_attn_in['Wo'], 'L0_attn_bo': _L0_attn_in['bo'], 'L0_attn_idx_k': _L0_attn_in['idx_k'], 'L0_ffn_w_freq_real': _L0_ffn_in['w_freq_real'], 'L0_ffn_w_freq_imag': _L0_ffn_in['w_freq_imag'], 'L0_ffn_bias': _L0_ffn_in['bias']}
    _x0 = _d['L0_attn_x']
    _d['L0_attn_x'] = jax.random.normal(jax.random.fold_in(jax.random.key(seed), 1), (16, 1024, 512), dtype=_x0.dtype)
    del _x0
    return _d

def reference(L0_attn_x, L0_attn_Wq, L0_attn_bq, L0_attn_Wk, L0_attn_bk, L0_attn_Wv, L0_attn_bv, L0_attn_Wo, L0_attn_bo, L0_attn_idx_k, L0_ffn_w_freq_real, L0_ffn_w_freq_imag, L0_ffn_bias):

    def _L0_attn_ref(x, Wq, bq, Wk, bk, Wv, bv, Wo, bo, idx_k):
        import math
        import jax, jax.numpy as jnp
        import numpy as np
        D_MODEL = 512
        NHEAD = 16
        DK = D_MODEL // NHEAD
        FACTOR = 5
        B, L = (4, 4096)
        U = max(1, min(FACTOR * math.ceil(math.log(L + 1)), L))
        Bv, Lv, _ = x.shape
        H, dk = (NHEAD, DK)
        u = idx_k.shape[0]
        scale = 1.0 / math.sqrt(dk)
        Q = (x @ Wq.T + bq).reshape(Bv, Lv, H, dk).transpose(0, 2, 1, 3)
        K = (x @ Wk.T + bk).reshape(Bv, Lv, H, dk).transpose(0, 2, 1, 3)
        V = (x @ Wv.T + bv).reshape(Bv, Lv, H, dk).transpose(0, 2, 1, 3)
        K_samp = K[:, :, idx_k, :]
        scores = jnp.einsum('bhld,bhud->bhlu', Q, K_samp) * scale
        M = scores.max(-1) - scores.mean(-1)
        _, top_idx = jax.lax.top_k(M, u)
        Q_top = jnp.take_along_axis(Q, top_idx[..., None], axis=2)
        attn = jax.nn.softmax(jnp.einsum('bhud,bhld->bhul', Q_top, K) * scale, axis=-1)
        ctx_top = jnp.einsum('bhul,bhld->bhud', attn, V)
        ctx = jnp.broadcast_to(V.mean(axis=2, keepdims=True), (Bv, H, Lv, dk))
        bidx = jnp.arange(Bv)[:, None, None]
        hidx = jnp.arange(H)[None, :, None]
        ctx = ctx.at[bidx, hidx, top_idx].set(ctx_top)
        ctx = ctx.transpose(0, 2, 1, 3).reshape(Bv, Lv, H * dk)
        return ctx @ Wo.T + bo

    def _L0_ffn_ref(x, w_freq_real, w_freq_imag, bias):
        import jax, jax.numpy as jnp
        import numpy as np
        B, N, D = (4, 1024, 512)
        SPARSITY = 0.01
        w = jax.lax.complex(w_freq_real, w_freq_imag)
        x_freq = jnp.fft.fft(x, axis=-1)
        y_freq = jnp.einsum('bnd,do->bno', x_freq, w)
        y = jnp.real(jnp.fft.ifft(y_freq, axis=-1))
        return y + bias
    x = L0_attn_x
    x = x + _L0_attn_ref(_layernorm(x, axis=-1), L0_attn_Wq, L0_attn_bq, L0_attn_Wk, L0_attn_bk, L0_attn_Wv, L0_attn_bv, L0_attn_Wo, L0_attn_bo, L0_attn_idx_k)
    x = x + _L0_ffn_ref(_layernorm(x, axis=-1), L0_ffn_w_freq_real, L0_ffn_w_freq_imag, L0_ffn_bias)
    return x

_drawn_inputs = setup_inputs


def setup_inputs(seed=0):
    import zlib

    import numpy as np

    out = dict(_drawn_inputs(seed))
    spreads = {'L0_attn_bq': (0.0, 0.8),
     'L0_attn_bk': (0.0, 0.8),
     'L0_attn_bv': (0.0, 0.1),
     'L0_attn_bo': (0.0, 0.1)}
    factors = {'L0_attn_Wq': 2.695, 'L0_ffn_bias': 8.0}
    for name, (base, spread) in spreads.items():
        noise = np.random.default_rng([zlib.crc32(name.encode()), seed]).standard_normal(out[name].shape)
        drawn = base * np.exp(spread * noise) if base else spread * noise
        out[name] = jnp.asarray(drawn.astype(out[name].dtype))
    for name, factor in factors.items():
        out[name] = (out[name] * factor).astype(out[name].dtype)
    return out
```

```python
from contextlib import ExitStack

import numpy as np

import concourse.bass as bass
from concourse import mybir

ALU = mybir.AluOpType
ACT = mybir.ActivationFunctionType
AX_X = mybir.AxisListType.X
F32 = mybir.dt.float32
F32R = mybir.dt.float32r
F16 = mybir.dt.float16
U32 = mybir.dt.uint32
I32 = mybir.dt.int32

P = 128
EPS = 1e-5
HI, LO = 0, 1
MARK = 2048.0

C_IDENT, C_HEAD, C_QHALF, C_DMASK, C_HROW, C_IDX0 = 0, 128, 132, 134, 198, 206
C_END = 214


def shapes_of(x, idx_k):
    B, L, D = x.shape
    H = 16
    U = idx_k.shape[0]
    return B, L, D, H, D // H, U


def constants(B, L, D, H, DK, U):
    HU = 2 * U
    BASE = (HU + 31) // 32 * 32
    c32 = np.zeros((P, C_END), np.float32)
    c32[:, C_IDENT:C_IDENT + P] = np.eye(P)
    for h in range(4):
        c32[h * DK:(h + 1) * DK, C_HEAD + h] = 1.0
    for a in range(2):
        c32[a * U:(a + 1) * U, C_QHALF + a] = 1.0
        c32[a * U:(a + 1) * U, C_DMASK + a * DK:C_DMASK + (a + 1) * DK] = 1.0
    c32[BASE, C_DMASK:C_DMASK + 2 * DK] = 1.0
    for p in range(H // 2):
        c32[:HU, C_HROW + p] = 2 * p + (np.arange(HU) >= U)
    c32[:, C_IDX0:C_IDX0 + H // 2] = -1.0
    c32[BASE, C_IDX0:C_IDX0 + H // 2] = MARK
    c16 = np.zeros((P, L + H * U + 2), np.float16)
    c16[:, :L] = np.arange(L)
    c16[BASE, :L] = MARK
    for h in range(H):
        c16[h, L + h * U:L + (h + 1) * U] = 1.0
    c16[:, L + H * U:] = 1.0
    k = np.arange(D)
    ang = 2.0 * np.pi * ((k[:, None] * k[None, :]) % D) / D
    trig = np.stack([np.cos(ang), np.sin(ang), -np.cos(ang)]).astype(np.float32)
    return c32, c16, trig


def column_tiles(bias):
    return np.ascontiguousarray(np.asarray(bias).reshape(-1, P).T)


def build(nc, x, wq, bq, wk, bk, wv, bv, wo, bo, idx_k, wfr, wfi, fbias, c32, c16, trig, out):
    B, L, D, H, DK, U = shapes_of(x, idx_k)
    LT = L // P
    CT = D // P
    HALF = 512
    NP_ = H // 2
    HU = 2 * U
    BASE = (HU + 31) // 32 * 32
    KR = BASE + 1
    SW = 4 * U + 4
    US = U + U % 2
    SCALE = float(DK) ** -0.5
    NN = LT + 1
    LAST = B - 1

    q_rows = nc.dram_tensor("q_rows", (L * H, DK), F32, kind="Internal").ap()
    q_by_row = q_rows.rearrange("(t p h) d -> p t (h d)", p=P, h=H)
    x_rows = x.rearrange("b l d -> (b l) d")

    ctx = ExitStack()
    with ctx:
        def sb(name, shape, dt):
            return ctx.enter_context(nc.sbuf_tensor(name, shape, dt))

        def early(name, shape, dt):
            with nc.sbuf_tensor(name, shape, dt) as t:
                return t

        def sem(name):
            return ctx.enter_context(nc.semaphore(name))

        W = {n: sb(f"w_{n}", [P, 2, CT, D], F32R) for n in ("q", "k", "v", "o", "g")}
        fin = early("fourier_inputs", [P, 4, CT, D], F32)
        xT = sb("xT", [P, 2, CT, L], F32R)
        kT = sb("kT", [P, 2, L], F32)
        v_x1 = sb("v_x1", [P, LT, D], F32)
        q_e = early("qT_qrow", [P, 4, 512], F32)
        oh = sb("onehot", [P, 2, L], F32R)
        stage = sb("stage", [P, 3, D], F32)
        xn1 = sb("xn1", [P, 3, D], F32)
        xn2 = sb("xn2", [P, 2, D], F32)
        prob = early("prob", [P, 2, L], F32)
        x2T = sb("x2T", [P, 2, 2, CT, P], F32R)
        pT = sb("pT", [P, 2, LT, BASE + 2], F32)
        cst = sb("cst", [P, C_END], F32)
        cst16 = sb("cst16", [P, L + H * U + 2], F16)
        mval = sb("mval", [P, LT, H], F32)
        mT = sb("mT", [H, L], F32)
        top_v = sb("top_v", [H, 48], F32)
        top_i = sb("top_i", [H, 48], U32)
        top_f = sb("top_f", [H, 48], F32)
        rsel = sb("rsel", [H, H, U], F16)
        idxc = sb("idxc", [P, NP_], F32)
        qidx = sb("qidx", [P, NP_], U32)
        qg = sb("qg", [P, NP_, DK], F32)
        qx = sb("qx", [P, 2, P], F32)
        qtT = sb("qtT", [P, NP_, HU], F32)
        xsT = sb("xsT", [P, 2, CT, US], F32R)
        ks = sb("ks", [P, CT, US], F32)
        kbd = sb("kbd", [P, CT, SW], F32)
        ksum = sb("ksum", [P, CT, 4], F32)
        dtmp = sb("dtmp", [P, 2, 2 * DK], F32)
        delta = sb("delta", [P, 2, 2, 2, P], F32R)
        bo_b = sb("bo_b", [P, D], F32)
        fb_b = sb("fb_b", [P, D], F32)
        bq_c = sb("bq_c", [P, CT], F32)
        bk_c = sb("bk_c", [P, CT], F32)
        bv_c = sb("bv_c", [P, CT], F32)
        sidx = sb("sidx", [P, 1], I32)
        soff = sb("soff", [P, 4], F32)
        soffu = sb("soffu", [P, 1], U32)
        mhalf = sb("mhalf", [P, 1], F32)
        bst = sb("bst", [P, 2, 6], F32)
        mv = [sb(f"mv{k}", [P, 9, 2], F32) for k in range(2)]
        vep = [sb(f"vep{k}", [P, 9], F32) for k in range(2)]
        rstd = [sb(f"rstd{k}", [P, 9], F32) for k in range(2)]
        negmax = sb("negmax", [P, 2, 2], F32)
        psum_ = sb("psum_", [P, 2, 2], F32)

        dense = [ctx.enter_context(nc.psum_tensor(f"dense{k}", [P, 512], F32)) for k in range(2)]
        turn = [ctx.enter_context(nc.psum_tensor(f"turn{k}", [P, 512], F32)) for k in range(2)]
        score = ctx.enter_context(nc.psum_tensor("score", [P, 4, 512], F32))

        ident = cst[:, C_IDENT:C_IDENT + P]

        consts_in = sem("consts_in")
        fourier_in = sem("fourier_in")
        weight_in = sem("weight_in")
        weight_hi = sem("weight_hi")
        weight_lo = sem("weight_lo")
        bias_in = sem("bias_in")
        g_full = sem("g_full")
        g_copied = sem("g_copied")
        g_hi = sem("g_hi")
        g_lo = sem("g_lo")
        bv_spread = sem("bv_spread")
        bo_full = sem("bo_full")
        bo_ready = sem("bo_ready")
        cleared = sem("cleared")
        soff_step = sem("soff_step")
        soff_ready = sem("soff_ready")
        sampled_in = sem("sampled_in")
        stage_in = [sem(f"stage_in{k}") for k in range(3)]
        bn_done = sem("bn_done")
        mean_ready = [sem(f"mean_ready{k}") for k in range(2)]
        eps_added = sem("eps_added")
        rstd_ready = [sem(f"rstd_ready{k}") for k in range(2)]
        norm_done = [sem(f"norm_done{k}") for k in range(2)]
        turn_full = sem("turn_full")
        dense_full = sem("dense_full")
        xT_hi = sem("xT_hi")
        xT_ready = sem("xT_ready")
        x2T_hi = sem("x2T_hi")
        x2T_ready = sem("x2T_ready")
        ks_ready = sem("ks_ready")
        kbd_step = sem("kbd_step")
        kbd_ready = sem("kbd_ready")
        qT_ready = sem("qT_ready")
        qrow_ready = sem("qrow_ready")
        q_stored = [sem(f"q_stored{k}") for k in range(2)]
        m_full = sem("m_full")
        m_max = sem("m_max")
        m_free = sem("m_free")
        mT_full = sem("mT_full")
        mT_ready = sem("mT_ready")
        top_max = sem("top_max")
        top_found = sem("top_found")
        top_struck = sem("top_struck")
        top_float = sem("top_float")
        rsel_ready = sem("rsel_ready")
        idx_full = sem("idx_full")
        idxc_ready = sem("idxc_ready")
        qidx_ready = sem("qidx_ready")
        q_gathered = [sem(f"q_gathered{k}") for k in range(NP_)]
        qx_ready = sem("qx_ready")
        qtT_ready = sem("qtT_ready")
        k_ready = sem("k_ready")
        v_ready = sem("v_ready")
        s_full = sem("s_full")
        s_max = sem("s_max")
        negmax_ready = sem("negmax_ready")
        exp_done = sem("exp_done")
        recip_done = sem("recip_done")
        prob_ready = sem("prob_ready")
        pT_ready = sem("pT_ready")
        dtmp_ready = sem("dtmp_ready")
        delta_hi = sem("delta_hi")
        delta_ready = sem("delta_ready")
        oh_ready = sem("oh_ready")
        ctx_hi = sem("ctx_hi")
        ctx_ready = sem("ctx_ready")
        xres_in = [sem(f"xres_in{k}") for k in range(LT)]
        bo_added = sem("bo_added")
        x1_ready = sem("x1_ready")
        fb_added = sem("fb_added")
        out_ready = sem("out_ready")
        out_stored = sem("out_stored")

        def turn_order(last):
            o = [("ks",)] + [("q", u) for u in range(8)] + [("qt", 0), ("qt", 1)]
            for p in range(NP_):
                if p + 2 < NP_:
                    o.append(("qt", p + 2))
                o += [("p", p, 0), ("p", p, 1)]
            o += [("x2", 0), ("x2", 1)]
            for t in range(LT):
                if t + 2 < LT:
                    o.append(("x2", t + 2))
                if not last:
                    o.append(("x", t))
            if not last:
                o.append(("x", LT))
            return o

        SCATTER_AT = {4: 0, 6: 1, 7: 2}

        def dense_order():
            o = [("q", u) for u in range(8)] + [("v", t) for t in range(LT)] + [("k", u) for u in range(4)]
            for p in range(NP_):
                if p < 4:
                    o.append(("k", 4 + p))
                if p >= 1:
                    o.append(("pv", p - 1))
                if p in SCATTER_AT:
                    o += [("sc", SCATTER_AT[p], h) for h in range(2)]
            o += [("pv", NP_ - 1), ("sc", 3, 0), ("sc", 3, 1)]
            o += [("o", t) for t in range(LT)] + [("f", t) for t in range(LT)]
            return o

        TURNS = {last: {k: n for n, k in enumerate(turn_order(last))} for last in (False, True)}
        DENSES = {k: n for n, k in enumerate(dense_order())}
        TPI, DPI = len(TURNS[False]), len(DENSES)
        assert TPI % 2 == 0 and DPI % 2 == 0

        def taken_of(RING, key, i):
            kind, n = key[0], (key[1] if len(key) > 1 else 0)
            return {
                ("d", "q"): lambda: (qT_ready, i * 8 + n + 1),
                ("d", "v"): lambda: (v_ready, i * LT + n + 1),
                ("d", "k"): lambda: (k_ready, i * 8 + n + 1),
                ("d", "pv"): lambda: (dtmp_ready, i * NP_ + n + 1),
                ("d", "sc"): lambda: (ctx_ready, i * 8 + 2 * n + key[2] + 1),
                ("d", "o"): lambda: (x1_ready, i * LT + n + 1),
                ("d", "f"): lambda: (out_ready, i * LT + n + 2),
                ("t", "ks"): lambda: (ks_ready, i + 1),
                ("t", "q"): lambda: (qrow_ready, i * 8 + n + 1),
                ("t", "qt"): lambda: (qtT_ready, i * NP_ + n + 1),
                ("t", "p"): lambda: (pT_ready, i * 2 * NP_ + 2 * n + key[2] + 1),
                ("t", "x2"): lambda: (x2T_ready, i * LT + n + 1),
                ("t", "x"): lambda: (xT_ready, i * NN + NN + n + 1),
            }[RING, kind]()

        class Use:
            def __init__(self, bank, free, full, full_at):
                self.bank, self.free, self.full, self.full_at = bank, free, full, full_at

        def turn_use(key, i, last):
            n = TURNS[last][key]
            names = list(TURNS[last])
            free = taken_of("t", names[n - 2], i) if n >= 2 else (xT_ready, i * NN + NN - 1 + n)
            return Use(turn[(NN + n) % 2], free, turn_full, i * TPI + NN + n + 1)

        def first_turn(n):
            return Use(turn[n % 2], (xT_ready, n - 1) if n >= 2 else None, turn_full, n + 1)

        def dense_use(key, i):
            n = DENSES[key]
            free = taken_of("d", list(DENSES)[n - 2], i) if n >= 2 else (out_ready, i * LT + 1)
            return Use(dense[n % 2], free, dense_full, i * DPI + n + 1)

        def samples(b):
            return lambda n: U if n == 0 else P

        rows_of = samples(0)

        def wait_stage(eng, i, b, n):
            if n == 0:
                eng.wait_ge(sampled_in, 16 * i + 16 * (b + 1))
            else:
                loads = 2 if n % 3 == 0 else 3
                nth = n // 3 - 1 if n % 3 == 0 else n // 3
                eng.wait_ge(stage_in[n % 3], 16 * loads * i + 16 * (loads * b + nth + 1))
        block = ctx.enter_context(nc.Block())

        @block.sync
        def _(sp):
            sp.sem_inc(out_stored, 16)
            sp.dma_start(cst[:, :], c32).then_inc(consts_in, 16)
            sp.dma_start(cst16[:, :], c16).then_inc(consts_in, 16)
            sp.dma_start(sidx[0:U, :], idx_k.rearrange("(u a) -> u a", a=1)).then_inc(consts_in, 16)
            for n, src in enumerate((wfr, trig[0], wfi, trig[1])):
                sp.dma_start(fin[:, (0, 2, 1, 3)[n]], src.rearrange("(c p) n -> p c n", p=P)).then_inc(fourier_in, 16)
            sp.dma_start(kT[:, :, :].rearrange("p a (b n) -> p (a b) n", n=D),
                         trig[2].rearrange("(c p) n -> p c n", p=P)).then_inc(fourier_in, 16)
            for src, dst in ((bq, bq_c), (bk, bk_c), (bv, bv_c)):
                sp.dma_start(dst[:, :], src).then_inc(bias_in, 16)
            for src, dst in ((bo, bo_b), (fbias, fb_b)):
                sp.dma_start(dst[:, :], src.partition_broadcast(P)).then_inc(bias_in, 16)
            for k in range(1, 3):
                sp.dma_start(stage[:, k, :], x[0, (k - 1) * P:k * P, :]).then_inc(stage_in[k], 16)
            for n, src in enumerate((wq, wk, wv, wo)):
                if n:
                    sp.wait_ge(weight_lo, n)
                sp.dma_start(prob[:, :, :].rearrange("p a (b n) -> p (a b) n", n=D),
                             src.rearrange("(c p) n -> p c n", p=P)).then_inc(weight_in, 16)
            for n in range(3, NN):
                sp.wait_ge(norm_done[0], n - 2)
                sp.dma_start(stage[:, n % 3, :], x[0, (n - 1) * P:n * P, :]).then_inc(stage_in[n % 3], 16)

            def batch(i, last):
                for u in range(8):
                    g, half = u // 2, u % 2
                    sp.wait_ge(qrow_ready, i * 8 + u + 1)
                    sp.dma_start(q_by_row[:, half * 4:half * 4 + 4, g * P:(g + 1) * P],
                                 q_e[:, 2 + u % 2, :].rearrange("p (t d) -> p t d", t=4)).then_inc(q_stored[u % 2], 16)
                sp.wait_ge(dense_full, dense_use(("pv", NP_ - 1), i).full_at)
                for t in range(LT):
                    sp.dma_start(v_x1[:, t, :], x[i, t * P:(t + 1) * P, :]).then_inc(xres_in[t], 16)
                if not last:
                    for n in range(1, 3):
                        sp.wait_ge(norm_done[0], i * NN + NN + n - 2)
                        sp.dma_start(stage[:, n, :], x[i + 1, (n - 1) * P:n * P, :]).then_inc(stage_in[n], 16)
                for t in range(LT):
                    if not last:
                        n = t + 3
                        if n < NN:
                            sp.wait_ge(norm_done[0], i * NN + NN + n - 2)
                            sp.dma_start(stage[:, n % 3, :],
                                         x[i + 1, (n - 1) * P:n * P, :]).then_inc(stage_in[n % 3], 16)
                    sp.wait_ge(out_ready, i * LT + t + 2)
                    sp.dma_start(out[i, t * P:(t + 1) * P, :], v_x1[:, t, :]).then_inc(out_stored, 16)

            with sp.Fori(0, LAST) as i:
                batch(i, False)
            batch(LAST, True)
            sp.wait_ge(out_stored, 16 * LT * B + 16)
            for k in range(2):
                sp.wait_ge(q_stored[k], 16 * 4 * B)

        def standing(eng):
            eng.nop(nofuse=True)

        @block.gpsimd
        def _(pool):
            pool.memset(mhalf[:, :], -0.5).then_inc(cleared, 1)
            pool.memset(pT[:, :, :, :], 0.0).then_inc(cleared, 1)
            pool.memset(qx[:, :, :], 0.0).then_inc(cleared, 1)
            pool.memset(delta[:, :, :, :, :].bitcast(F32), 0.0).then_inc(cleared, 1)
            pool.memset(xsT[:, :, :, :].bitcast(F32), 0.0).then_inc(cleared, 1)
            pool.wait_ge(cleared, 5)
            pool.memset(pT[:, :, :, BASE:BASE + 1], 1.0 / L).then_inc(cleared, 1)

            def sample_rows(b):
                pool.wait_ge(soff_ready, b + 1)
                standing(pool)
                pool.indirect_dma_start(stage[0:U, 0, :], None, x_rows[:, :],
                                        bass.IndirectOffsetOnAxis(ap=soffu[0:U, 0:1], axis=0)).then_inc(sampled_in, 16)

            npow = [0]

            def power(which, count, n, rows):
                pool.wait_ge(mean_ready[which], count + 1)
                standing(pool)
                pool.tensor_scalar(vep[which][0:rows, n:n + 1], mv[which][0:rows, n, 1:2], EPS, 1.0,
                                   ALU.add, ALU.mult).then_inc(eps_added, 1)

            def power2(which, n, rows, adds):
                pool.wait_ge(eps_added, adds)
                pool.tensor_tensor(rstd[which][0:rows, n:n + 1], vep[which][0:rows, n:n + 1],
                                   mhalf[0:rows, :], ALU.pow).then_inc(rstd_ready[which], 1)

            sample_rows(0)
            for n in range(NN):
                power(0, n, n, rows_of(n))
                power2(0, n, rows_of(n), n + 1)
            PER = NN + LT

            def batch(i, last):
                adds = [0]

                def rstd1(n):
                    if last:
                        return
                    power(0, i * NN + NN + n, n, rows_of(n))
                    adds[0] += 1
                    power2(0, n, rows_of(n), i * PER + NN + adds[0])

                def rstd2(t):
                    power(1, i * LT + t, t, P)
                    adds[0] += 1
                    power2(1, t, P, i * PER + NN + adds[0])

                def add_fb(t):
                    pool.wait_ge(norm_done[1], i * LT + t + 1)
                    pool.tensor_tensor(v_x1[:, t, :], v_x1[:, t, :], fb_b[:, :], ALU.add).then_inc(fb_added, 1)

                for s in range(2):
                    pool.wait_ge(q_stored[s], i * 64 + 64)
                pool.wait_ge(qidx_ready, i + 1)
                standing(pool)
                for p in range(NP_):
                    pool.indirect_dma_start(qg[0:HU, p, :], None, q_rows[:, :],
                                            bass.IndirectOffsetOnAxis(ap=qidx[0:HU, p:p + 1], axis=0)
                                            ).then_inc(q_gathered[p], 16)
                if not last:
                    pool.wait_ge(norm_done[0], i * NN + NN - 2)
                    sample_rows(i + 1)
                if not last:
                    pass
                for t in range(LT):
                    pool.wait_ge(xres_in[t], i * 16 + 16)
                    if t == 0:
                        pool.wait_ge(bo_ready, 1)
                    pool.tensor_tensor(v_x1[:, t, :], v_x1[:, t, :], bo_b[:, :], ALU.add).then_inc(bo_added, 1)
                rstd2(0), rstd2(1), rstd1(0), rstd2(2), rstd1(1), rstd2(3), rstd1(2), rstd2(4)
                add_fb(0), rstd2(5), rstd1(3), add_fb(1), rstd2(6), rstd2(7), add_fb(2), add_fb(3)
                for t in range(LT):
                    if t + 4 < NN:
                        rstd1(t + 4)
                    if t + 4 < LT:
                        add_fb(t + 4)

            with pool.Fori(0, LAST) as i:
                batch(i, False)
            batch(LAST, True)

        @block.scalar
        def _(act):
            def wstage():
                return prob[:, :, :].rearrange("p a (b n) -> p (a b) n", n=D)

            for n, w in enumerate("qkvo"):
                act.wait_ge(weight_in, 16 * (n + 1))
                nc.scalar.activation(W[w][:, HI], wstage(), ACT.Copy).then_inc(weight_hi, 1)
            for n in range(8):
                act.wait_ge(g_full, n + 1)
                nc.scalar.activation(v_x1[:, n, :], score[:, n % 4, :], ACT.Copy).then_inc(g_copied, 1)
            for n in range(4):
                act.wait_ge(g_full, 9 + n)
                nc.scalar.activation(W["g"][:, HI, n, :], score[:, n, :], ACT.Copy, scale=1.0 / D).then_inc(g_hi, 1)

            def hi_of_turn(u, dst, done):
                act.wait_ge(turn_full, u.full_at)
                nc.scalar.activation(dst, u.bank[:, :].rearrange("p (c l) -> p c l", c=CT)[:, :, 0:dst.shape[-1]],
                                     ACT.Copy).then_inc(done, 1)

            def xT_dst(n):
                return xsT[:, HI, :, 0:U] if n == 0 else xT[:, HI, :, (n - 1) * P:n * P]

            act.wait_ge(cleared, 6)
            for n in range(NN):
                hi_of_turn(first_turn(n), xT_dst(n), xT_hi)

            def batch(i, last):
                T = lambda *k: turn_use(k, i, last)
                Dn = lambda *k: dense_use(k, i)
                u = T("ks")
                act.wait_ge(turn_full, u.full_at)
                for g in range(CT):
                    a = nc.scalar.activation(ks[:, g, :], u.bank[:, g * P:g * P + US], ACT.Identity,
                                             bias=bk_c[:, g:g + 1])
                    if g == CT - 1:
                        a.then_inc(ks_ready, 1)

                def q_out(n):
                    d = Dn("q", n)
                    act.wait_ge(dense_full, d.full_at)
                    if n >= 2:
                        act.wait_ge(turn_full, T("q", n - 2).full_at)
                    nc.scalar.activation(q_e[:, n % 2, :], d.bank[:, :], ACT.Identity,
                                         bias=bq_c[:, n // 2:n // 2 + 1]).then_inc(qT_ready, 1)

                def qrow_out(n):
                    d = T("q", n)
                    act.wait_ge(turn_full, d.full_at)
                    if n >= 2:
                        act.wait_ge(q_stored[n % 2], i * 64 + 16 * (n // 2))
                    nc.scalar.activation(q_e[:, 2 + n % 2, :], d.bank[:, :], ACT.Copy).then_inc(qrow_ready, 1)

                q_out(0)
                for n in range(1, 8):
                    q_out(n)
                    qrow_out(n - 1)
                qrow_out(7)

                def v_out(t):
                    d = Dn("v", t)
                    act.wait_ge(dense_full, d.full_at)
                    if t == 0:
                        act.wait_ge(out_stored, i * 16 * LT + 16)
                    nc.scalar.activation(v_x1[:, t, :], d.bank[:, :], ACT.Copy).then_inc(v_ready, 1)

                v_out(0)
                act.wait_ge(mT_full, i + 1)
                nc.scalar.activation(mT[:, :], score[0:H, 0:2, :], ACT.Copy).then_inc(mT_ready, 1)
                for t in range(1, LT):
                    v_out(t)

                def k_out(n):
                    d = Dn("k", n)
                    g, half = n // 2, n % 2
                    act.wait_ge(dense_full, d.full_at)
                    nc.scalar.activation(kT[:, g % 2, half * 512:half * 512 + 512], d.bank[:, :], ACT.Identity,
                                         bias=bk_c[:, g:g + 1]).then_inc(k_ready, 1)

                def qt_out(p):
                    u = T("qt", p)
                    act.wait_ge(turn_full, u.full_at)
                    nc.scalar.activation(qtT[:, p, :], u.bank[:, 0:HU], ACT.Copy).then_inc(qtT_ready, 1)

                def exps(p):
                    act.wait_ge(negmax_ready, i * NP_ + p + 1)
                    if p >= 2:
                        act.wait_ge(turn_full, T("p", p - 2, 1).full_at)
                    nc.scalar.activation(prob[0:HU, p % 2, :], score[0:HU, 2 * (p % 2):2 * (p % 2) + 2, :], ACT.Exp,
                                         bias=negmax[0:HU, p % 2, 1:2], scale=SCALE,
                                         accum_out=psum_[0:HU, p % 2, 0:1]).then_inc(exp_done, 1)

                def pT_out(p):
                    for h in range(2):
                        u = T("p", p, h)
                        act.wait_ge(turn_full, u.full_at)
                        nc.scalar.activation(pT[:, p % 2, 4 * h:4 * h + 4, 0:HU],
                                             u.bank[:, :].rearrange("p (t r) -> p t r", t=4)[:, :, 0:HU],
                                             ACT.Copy).then_inc(pT_ready, 1)

                def sc_out(g):
                    for h in range(2):
                        d = Dn("sc", g, h)
                        act.wait_ge(dense_full, d.full_at)
                        nc.scalar.activation(xT[:, HI, g, h * 512:h * 512 + 512], d.bank[:, :],
                                             ACT.Copy).then_inc(ctx_hi, 1)

                for n in range(4):
                    k_out(n)
                qt_out(0)
                qt_out(1)
                exps(0)
                for p in range(NP_):
                    if p + 2 < NP_:
                        qt_out(p + 2)
                    if p + 1 < NP_:
                        exps(p + 1)
                    if p < 4:
                        k_out(4 + p)
                    pT_out(p)
                    if p in SCATTER_AT:
                        sc_out(SCATTER_AT[p])
                sc_out(3)

                def x2_out(t):
                    hi_of_turn(T("x2", t), x2T[:, t % 2, HI, :, :], x2T_hi)

                x2_out(0)
                x2_out(1)
                for t in range(LT):
                    if t + 2 < LT:
                        x2_out(t + 2)
                    if not last:
                        hi_of_turn(T("x", t), xT_dst(t), xT_hi)
                if not last:
                    hi_of_turn(T("x", LT), xT_dst(LT), xT_hi)

            with act.Fori(0, LAST) as i:
                batch(i, False)
            batch(LAST, True)

        @block.tensor
        def _(pe):
            mm = nc.tensor.matmul

            def three_pass(dst, pairs, wait=None):
                todo = [(l[a], r[b]) for l, r in pairs for a, b in ((HI, HI), (HI, LO), (LO, HI))]
                for n, (l, r) in enumerate(todo):
                    if wait and n in wait:
                        pe.wait_ge(*wait[n])
                    m = mm(dst, l, r, start=(n == 0), stop=(n == len(todo) - 1))
                return m

            wr_, wi_, cos_, sin_ = (fin[:, k] for k in range(4))
            ncos = kT[:, :, :].rearrange("p a (b n) -> p (a b) n", n=D)
            pe.wait_ge(fourier_in, 80)
            for n in range(8):
                if n >= 4:
                    pe.wait_ge(g_copied, n - 3)
                o = n % 4
                for c in range(CT):
                    for w, t in ((wr_, cos_ if n < 4 else sin_), (wi_, sin_ if n < 4 else ncos)):
                        m = mm(score[:, n % 4, :], w[:, c, o * P:(o + 1) * P], t[:, c, :],
                               start=(c == 0 and w is wr_), stop=(c == CT - 1 and w is wi_))
                m.then_inc(g_full, 1)
            pe.wait_ge(g_copied, 8)
            for n in range(4):
                for o in range(CT):
                    for k, t in ((0, cos_), (1, sin_)):
                        m = mm(score[:, n, :], v_x1[:, 4 * k + o, n * P:(n + 1) * P], t[:, o, :],
                               start=(o == 0 and k == 0), stop=(o == CT - 1 and k == 1))
                m.then_inc(g_full, 1)
            pe.wait_ge(bv_spread, 1)
            pe.wait_ge(weight_in, 64)
            pe.wait_ge(g_lo, 1)
            for c in range(CT):
                m = mm(score[:, 0, :], qtT[:, :, :].rearrange("p a b -> p (a b)")[:, c * P:(c + 1) * P],
                       prob[:, c // 2, (c % 2) * 512:(c % 2) * 512 + 512], start=(c == 0), stop=(c == CT - 1))
            m.then_inc(bo_full, 1)

            def turn_tile(u, src, rows, ncol=CT):
                if u.free:
                    pe.wait_ge(*u.free)
                if rows < P:
                    standing(pe)
                for c in range(ncol):
                    m = nc.tensor.transpose(u.bank[:, c * P:c * P + rows], src[0:rows, c * P:(c + 1) * P],
                                            ident[0:rows, 0:rows])
                m.then_inc(turn_full, 1)

            pe.wait_ge(consts_in, 48)
            for n in range(NN):
                pe.wait_ge(norm_done[0], n + 1)
                turn_tile(first_turn(n), xn1[:, n % 3, :], rows_of(n))

            def batch(i, last):
                T = lambda *k: turn_use(k, i, last)
                Dn = lambda *k: dense_use(k, i)

                u = T("ks")
                pe.wait_ge(*u.free)
                pe.wait_ge(xT_ready, i * NN + 1)
                for g in range(CT):
                    m = three_pass(u.bank[:, g * P:g * P + US],
                                   [([W["k"][:, a, c, g * P:(g + 1) * P] for a in (HI, LO)],
                                     [xsT[:, a, c, :] for a in (HI, LO)]) for c in range(CT)])
                m.then_inc(turn_full, 1)

                def q_proj(n):
                    g, half = n // 2, n % 2
                    d = Dn("q", n)
                    pe.wait_ge(*d.free)
                    if n < 2:
                        pe.wait_ge(xT_ready, i * NN + 1 + 4 * (half + 1))
                    three_pass(d.bank[:, :],
                               [([W["q"][:, a, c, g * P:(g + 1) * P] for a in (HI, LO)],
                                 [xT[:, a, c, half * 512:half * 512 + 512] for a in (HI, LO)])
                                for c in range(CT)]).then_inc(dense_full, 1)

                def q_use(n):
                    g = n // 2
                    pe.wait_ge(qT_ready, i * 8 + n + 1)
                    if n == 0:
                        pe.wait_ge(kbd_ready, i + 1)
                    for b in range(2):
                        use = 2 * n + b
                        if use >= 4:
                            pe.wait_ge(m_free, i * 16 + use - 3)
                        for k in range(2):
                            m = mm(score[:, use % 4, k * SW:(k + 1) * SW],
                                   q_e[:, n % 2, (2 * b + k) * P:(2 * b + k + 1) * P], kbd[:, g, :],
                                   start=True, stop=True)
                        m.then_inc(m_full, 1)
                    turn_tile(T("q", n), q_e[:, n % 2, :], P)

                q_proj(0)
                for n in range(1, 8):
                    q_proj(n)
                    q_use(n - 1)
                q_use(7)

                def v_proj(t):
                    d = Dn("v", t)
                    pe.wait_ge(*d.free)
                    three_pass(d.bank[:, :],
                               [([xT[:, a, c, t * P:(t + 1) * P] for a in (HI, LO)],
                                 [W["v"][:, a, c, :] for a in (HI, LO)]) for c in range(CT)]).then_inc(dense_full, 1)

                def k_proj(n):
                    g, half = n // 2, n % 2
                    d = Dn("k", n)
                    pe.wait_ge(*d.free)
                    three_pass(d.bank[:, :],
                               [([W["k"][:, a, c, g * P:(g + 1) * P] for a in (HI, LO)],
                                 [xT[:, a, c, half * 512:half * 512 + 512] for a in (HI, LO)])
                                for c in range(CT)]).then_inc(dense_full, 1)

                v_proj(0)
                pe.wait_ge(m_free, i * 16 + 16)
                for t in range(LT):
                    m = nc.tensor.transpose(score[0:H, t // 4, (t % 4) * P:(t % 4 + 1) * P], mval[:, t, :], ident)
                m.then_inc(mT_full, 1)
                for t in range(1, LT):
                    v_proj(t)
                for n in range(2):
                    k_proj(n)
                pe.wait_ge(rsel_ready, i + 1)
                for p in range(NP_):
                    m = mm(score[0:HU, 2, 2 * p:2 * p + 2],
                           rsel[:, 2 * p:2 * p + 2, :].rearrange("h a u -> h (a u)"),
                           cst16[0:H, L + H * U:L + H * U + 2], start=True, stop=True)
                m.then_inc(idx_full, 1)
                for n in range(2, 4):
                    k_proj(n)

                def qt_turn(p):
                    u = T("qt", p)
                    pe.wait_ge(*u.free)
                    pe.wait_ge(qx_ready, i * NP_ + p + 1)
                    nc.tensor.transpose(u.bank[:, 0:HU], qx[0:HU, p % 2, :], ident[0:HU, 0:HU]).then_inc(turn_full, 1)

                def qk(p):
                    g = p // 2
                    pe.wait_ge(qtT_ready, i * NP_ + p + 1)
                    pe.wait_ge(k_ready, i * 8 + 2 * g + 2)
                    if p >= 2:
                        pe.wait_ge(exp_done, i * NP_ + p - 1)
                    for h in range(2):
                        m = mm(score[0:HU, 2 * (p % 2) + h, :], qtT[:, p, :], kT[:, g % 2, h * 512:h * 512 + 512],
                               start=True, stop=True)
                    m.then_inc(s_full, 1)

                def p_turn(p):
                    pe.wait_ge(prob_ready, i * NP_ + p + 1)
                    for h in range(2):
                        u = T("p", p, h)
                        pe.wait_ge(*u.free)
                        for t in range(4):
                            m = nc.tensor.transpose(u.bank[:, t * P:t * P + HU],
                                                    prob[0:HU, p % 2, (4 * h + t) * P:(4 * h + t + 1) * P],
                                                    ident[0:HU, 0:HU])
                        m.then_inc(turn_full, 1)

                def pv(p):
                    d = Dn("pv", p)
                    pe.wait_ge(*d.free)
                    pe.wait_ge(pT_ready, i * 2 * NP_ + 2 * p + 2)
                    if p == 0:
                        pe.wait_ge(v_ready, i * LT + LT)
                    for t in range(LT):
                        m = mm(d.bank[0:KR, 0:2 * DK], pT[:, p % 2, t, 0:KR], v_x1[:, t, p * 2 * DK:(p + 1) * 2 * DK],
                               start=(t == 0), stop=(t == LT - 1))
                    m.then_inc(dense_full, 1)

                def scatter(g):
                    pe.wait_ge(delta_ready, i * NP_ + 2 * g + 2)
                    pe.wait_ge(oh_ready, i * NP_ + 2 * g + 2)
                    for h in range(2):
                        d = Dn("sc", g, h)
                        pe.wait_ge(*d.free)
                        for n, (e, a) in enumerate(((0, HI), (0, LO), (1, HI), (1, LO))):
                            m = mm(d.bank[:, :], delta[0:KR, g % 2, e, a, :], oh[0:KR, e, h * 512:h * 512 + 512],
                                   start=(n == 0), stop=(n == 3))
                        m.then_inc(dense_full, 1)

                qt_turn(0)
                qt_turn(1)
                qk(0)
                for p in range(NP_):
                    if p + 2 < NP_:
                        qt_turn(p + 2)
                    if p + 1 < NP_:
                        qk(p + 1)
                    if p < 4:
                        k_proj(4 + p)
                    p_turn(p)
                    if p >= 1:
                        pv(p - 1)
                    if p in SCATTER_AT:
                        scatter(SCATTER_AT[p])
                pv(NP_ - 1)
                scatter(3)

                def o_proj(t):
                    d = Dn("o", t)
                    pe.wait_ge(*d.free)
                    wait = None
                    if t % 4 == 0:
                        wait = {0: (ctx_ready, i * 8 + 6), 9: (ctx_ready, i * 8 + 7 + t // 4)}
                    three_pass(d.bank[:, :],
                               [([xT[:, a, g, t * P:(t + 1) * P] for a in (HI, LO)],
                                 [W["o"][:, a, g, :] for a in (HI, LO)]) for g in range(CT)], wait
                               ).then_inc(dense_full, 1)

                def x2_turn(t):
                    pe.wait_ge(norm_done[1], i * LT + t + 1)
                    turn_tile(T("x2", t), xn2[:, t % 2, :], P)

                def x_turn(n):
                    pe.wait_ge(norm_done[0], i * NN + NN + n + 1)
                    turn_tile(T("x", n), xn1[:, n % 3, :], rows_of(n))

                def fourier(t):
                    d = Dn("f", t)
                    pe.wait_ge(*d.free)
                    pe.wait_ge(x2T_ready, i * LT + t + 1)
                    three_pass(d.bank[:, :],
                               [([x2T[:, t % 2, a, c, :] for a in (HI, LO)],
                                 [W["g"][:, a, c, :] for a in (HI, LO)]) for c in range(CT)]).then_inc(dense_full, 1)

                for t in range(6):
                    o_proj(t)
                x2_turn(0)
                o_proj(6)
                x2_turn(1)
                o_proj(7)
                for t in range(LT):
                    fourier(t)
                    if t + 2 < LT:
                        x2_turn(t + 2)
                    if not last:
                        x_turn(t)
                if not last:
                    x_turn(LT)

            pe.wait_ge(weight_lo, 4)
            pe.wait_ge(g_lo, 4)
            with pe.Fori(0, LAST) as i:
                batch(i, False)
            batch(LAST, True)

        @block.vector
        def _(dve):
            v = nc.vector
            bns = [0]

            def stats(which, count, n, src, rows, nth):
                v.bn_stats(bst[0:rows, which, :], src)
                dve.drain()
                v.bn_aggr(mv[which][0:rows, n, :], bst[0:rows, which, :]).then_inc(mean_ready[which], 1)

            def normalise(which, count, n, src, dst, rows):
                dve.wait_ge(rstd_ready[which], count + 1)
                v.tensor_scalar(dst, src, mv[which][0:rows, n, 0:1], rstd[which][0:rows, n:n + 1],
                                ALU.subtract, ALU.mult).then_inc(norm_done[which], 1)

            def stats1(n, nth):
                wait_stage(dve, 0, 0, n)
                stats(0, n, n, stage[0:rows_of(n), n % 3, :], rows_of(n), nth)

            def norm1(b9, n, turned):
                if turned is not None:
                    dve.wait_ge(turn_full, turned)
                normalise(0, b9 + n, n, stage[0:rows_of(n), n % 3, :], xn1[0:rows_of(n), n % 3, :], rows_of(n))

            def xT_lo(u, n, b9):
                hi, dst = ((xsT[:, a, :, 0:U] if n == 0 else xT[:, a, :, (n - 1) * P:n * P]) for a in (HI, LO))
                dve.wait_ge(xT_hi, b9 + n + 1)
                v.tensor_tensor(dst, u.bank[:, :].rearrange("p (c l) -> p c l", c=CT)[:, :, 0:dst.shape[-1]],
                                hi.bitcast(F32), ALU.subtract).then_inc(xT_ready, 1)

            dve.sem_inc(out_ready, 1)
            dve.wait_ge(consts_in, 48)
            v.tensor_copy(soff[0:U, 0:1], sidx[0:U, :]).then_inc(soff_step, 1)
            dve.wait_ge(soff_step, 1)
            v.tensor_scalar(soff[0:U, 1:2], soff[0:U, 0:1], 0.0, float(L), ALU.is_lt, ALU.mult).then_inc(soff_step, 1)
            dve.wait_ge(soff_step, 2)
            v.tensor_tensor(soff[0:U, 2:3], soff[0:U, 0:1], soff[0:U, 1:2], ALU.add).then_inc(soff_step, 1)
            dve.wait_ge(soff_step, 3)
            v.tensor_scalar(soff[0:U, 3:4], soff[0:U, 2:3], 0.0, float(L - 1), ALU.max, ALU.min).then_inc(soff_step, 1)
            dve.wait_ge(soff_step, 4)
            v.tensor_copy(soffu[0:U, :], soff[0:U, 3:4]).then_inc(soff_ready, 1)
            v.tensor_copy(idxc[:, :], cst[:, C_IDX0:C_IDX0 + NP_]).then_inc(soff_step, 1)
            dve.wait_ge(bias_in, 80)
            for c in range(CT):
                m = v.tensor_copy(qtT[:, :, :].rearrange("p a b -> p (a b)")[:, c * P:(c + 1) * P],
                                  bv_c[:, c:c + 1].broadcast_to([P, P]))
            m.then_inc(bv_spread, 1)
            for n, w in enumerate("qkvo"):
                dve.wait_ge(weight_hi, n + 1)
                v.tensor_tensor(W[w][:, LO], prob[:, :, :].rearrange("p a (b n) -> p (a b) n", n=D),
                                W[w][:, HI].bitcast(F32), ALU.subtract).then_inc(weight_lo, 1)
            for n in range(3):
                stats1(n, n)
                norm1(0, n, None)
            for n in range(4):
                dve.wait_ge(g_hi, n + 1)
                v.scalar_tensor_tensor(W["g"][:, LO, n, :], score[:, n, :], 1.0 / D, W["g"][:, HI, n, :].bitcast(F32),
                                       ALU.mult, ALU.subtract).then_inc(g_lo, 1)
            dve.wait_ge(bo_full, 1)
            v.tensor_tensor(bo_b[:, :], score[:, 0, :], bo_b[:, :], ALU.add).then_inc(bo_ready, 1)
            for n in range(NN):
                xT_lo(first_turn(n), n, 0)
                if n + 3 < NN:
                    stats1(n + 3, n + 3)
                    norm1(0, n + 3, first_turn(n).full_at)

            def batch(i, last):
                T = lambda *k: turn_use(k, i, last)
                Dn = lambda *k: dense_use(k, i)
                per_bn = NN + LT

                if not last:
                    dve.wait_ge(sampled_in, 16 * i + 16)
                    v.tensor_scalar(soff[0:U, 3:4], soff[0:U, 3:4], float(L), None, ALU.add).then_inc(soff_step, 1)
                    dve.wait_ge(soff_step, i + 6)
                    v.tensor_copy(soffu[0:U, :], soff[0:U, 3:4]).then_inc(soff_ready, 1)

                dve.wait_ge(ks_ready, i + 1)
                for h in range(4):
                    v.tensor_scalar(kbd[:, :, h * U:(h + 1) * U], ks[:, :, 0:U], cst[:, C_HEAD + h:C_HEAD + h + 1],
                                    SCALE, ALU.mult, ALU.mult).then_inc(kbd_step, 1)
                dve.wait_ge(kbd_step, i * 5 + 4)
                v.tensor_reduce(ksum[:, :, :], kbd[:, :, 0:4 * U].rearrange("p g (h u) -> p g h u", h=4), AX_X,
                                ALU.add).then_inc(kbd_step, 1)
                dve.wait_ge(kbd_step, i * 5 + 5)
                v.tensor_scalar(kbd[:, :, 4 * U:SW], ksum[:, :, :], 1.0 / U, None, ALU.mult).then_inc(kbd_ready, 1)

                for n in range(8):
                    g, half = n // 2, n % 2
                    for b in range(2):
                        use = 2 * n + b
                        t0 = half * 4 + 2 * b
                        s = score[:, use % 4, 0:2 * SW].rearrange("p (t k) -> p t k", t=2)
                        dve.wait_ge(m_full, i * 16 + use + 1)
                        mslot = mval[:, t0:t0 + 2, 4 * g:4 * g + 4]
                        v.tensor_reduce(mslot, s[:, :, 0:4 * U].rearrange("p t (h u) -> p t h u", h=4), AX_X,
                                        ALU.max).then_inc(m_max, 1)
                        dve.wait_ge(m_max, i * 16 + use + 1)
                        v.tensor_tensor(mslot, mslot, s[:, :, 4 * U:SW], ALU.subtract).then_inc(m_free, 1)

                dve.wait_ge(mT_ready, i + 1)
                for r in range(6):
                    r8 = slice(8 * r, 8 * r + 8)
                    if r == 0:
                        standing(dve)
                    else:
                        dve.drain()
                    v.max(top_v[:, r8], mT[:, :])
                    dve.drain()
                    m = v.max_index(top_i[:, r8], top_v[:, r8], mT[:, :])
                    if r < 5:
                        dve.drain()
                        v.match_replace(mT[:, :], top_v[:, r8], mT[:, :], -3.0e38)
                m.then_inc(top_found, 1)
                dve.wait_ge(top_found, i + 1)
                v.tensor_copy(top_f[:, :], top_i[:, :]).then_inc(top_float, 1)
                dve.wait_ge(top_float, i + 1)
                v.tensor_tensor(rsel[:, :, :], top_f[:, 0:U].unsqueeze(1).broadcast_to([H, H, U]),
                                cst16[0:H, L:L + H * U].rearrange("h (a u) -> h a u", a=H), ALU.mult
                                ).then_inc(rsel_ready, 1)
                dve.wait_ge(idx_full, i + 1)
                cols = score[0:HU, 2, 0:2 * NP_].rearrange("r (p two) -> r p two", two=2)[:, :, 0]
                v.tensor_copy(idxc[0:HU, :], cols).then_inc(idxc_ready, 1)
                v.scalar_tensor_tensor(qidx[0:HU, :], cols, float(H), cst[0:HU, C_HROW:C_HROW + NP_], ALU.mult,
                                       ALU.add).then_inc(qidx_ready, 1)

                def spread_q(p):
                    e = p % 2
                    dve.wait_ge(q_gathered[p], i * 16 + 16)
                    if p >= 2:
                        dve.wait_ge(turn_full, T("qt", p - 2).full_at)
                    for a in range(2):
                        m = v.tensor_scalar(qx[0:HU, e, (2 * e + a) * DK:(2 * e + a + 1) * DK], qg[0:HU, p, :],
                                            cst[0:HU, C_QHALF + a:C_QHALF + a + 1], None, ALU.mult)
                    m.then_inc(qx_ready, 1)

                def onehot(p):
                    if p == 0:
                        dve.wait_ge(idxc_ready, i + 1)
                    if p >= 2:
                        dve.wait_ge(dense_full, Dn("sc", p // 2 - 1, 1).full_at)
                    v.tensor_scalar(oh[0:KR, p % 2, :], cst16[0:KR, 0:L], idxc[0:KR, p:p + 1], None,
                                    ALU.is_equal).then_inc(oh_ready, 1)

                def row_max(p):
                    dve.wait_ge(s_full, i * NP_ + p + 1)
                    v.tensor_reduce(negmax[0:HU, p % 2, 0:1], score[0:HU, 2 * (p % 2):2 * (p % 2) + 2, :],
                                    mybir.AxisListType.XY, ALU.max).then_inc(s_max, 1)
                    dve.wait_ge(s_max, i * NP_ + p + 1)
                    v.tensor_scalar(negmax[0:HU, p % 2, 1:2], negmax[0:HU, p % 2, 0:1], -SCALE, None,
                                    ALU.mult).then_inc(negmax_ready, 1)

                def weights(p):
                    dve.wait_ge(exp_done, i * NP_ + p + 1)
                    v.reciprocal(psum_[0:HU, p % 2, 1:2], psum_[0:HU, p % 2, 0:1]).then_inc(recip_done, 1)
                    dve.wait_ge(recip_done, i * NP_ + p + 1)
                    v.tensor_scalar(prob[0:HU, p % 2, :], prob[0:HU, p % 2, :], psum_[0:HU, p % 2, 1:2], -1.0 / L,
                                    ALU.mult, ALU.add).then_inc(prob_ready, 1)

                def delta_of(p):
                    g, e = p // 2, p % 2
                    d = Dn("pv", p)
                    cols_ = slice(e * 2 * DK, (e + 1) * 2 * DK)
                    dve.wait_ge(dense_full, d.full_at)
                    v.tensor_tensor(dtmp[0:KR, e, :], d.bank[0:KR, 0:2 * DK], cst[0:KR, C_DMASK:C_DMASK + 2 * DK],
                                    ALU.mult).then_inc(dtmp_ready, 1)
                    dve.wait_ge(dtmp_ready, i * NP_ + p + 1)
                    v.tensor_copy(delta[0:KR, g % 2, e, HI, cols_], dtmp[0:KR, e, :]).then_inc(delta_hi, 1)
                    dve.wait_ge(delta_hi, i * NP_ + p + 1)
                    v.tensor_tensor(delta[0:KR, g % 2, e, LO, cols_], dtmp[0:KR, e, :],
                                    delta[0:KR, g % 2, e, HI, cols_].bitcast(F32), ALU.subtract).then_inc(delta_ready, 1)

                def ctx_lo(g):
                    for h in range(2):
                        d = Dn("sc", g, h)
                        cols_ = slice(h * 512, h * 512 + 512)
                        dve.wait_ge(ctx_hi, i * 8 + 2 * g + h + 1)
                        v.tensor_tensor(xT[:, LO, g, cols_], d.bank[:, :], xT[:, HI, g, cols_].bitcast(F32),
                                        ALU.subtract).then_inc(ctx_ready, 1)

                spread_q(0)
                spread_q(1)
                onehot(0)
                onehot(1)
                row_max(0)
                for p in range(NP_):
                    if p + 2 < NP_:
                        spread_q(p + 2)
                    weights(p)
                    if p + 1 < NP_:
                        row_max(p + 1)
                    if p >= 1:
                        delta_of(p - 1)
                    if p in SCATTER_AT:
                        g = SCATTER_AT[p]
                        ctx_lo(g)
                        onehot(2 * g + 2)
                        onehot(2 * g + 3)
                delta_of(NP_ - 1)
                ctx_lo(3)

                nth = [0]

                def st(which, n, src, rows):
                    stats(which, 0, n, src, rows, i * per_bn + NN + nth[0])
                    nth[0] += 1

                def res1(t):
                    d = Dn("o", t)
                    dve.wait_ge(dense_full, d.full_at)
                    dve.wait_ge(bo_added, i * LT + t + 1)
                    v.tensor_tensor(v_x1[:, t, :], d.bank[:, :], v_x1[:, t, :], ALU.add).then_inc(x1_ready, 1)
                    dve.wait_ge(x1_ready, i * LT + t + 1)
                    st(1, t, v_x1[:, t, :], P)

                def norm2(t):
                    if t >= 2:
                        dve.wait_ge(turn_full, T("x2", t - 2).full_at)
                    normalise(1, i * LT + t, t, v_x1[:, t, :], xn2[:, t % 2, :], P)

                def x2_lo(t):
                    u = T("x2", t)
                    dve.wait_ge(x2T_hi, i * LT + t + 1)
                    v.tensor_tensor(x2T[:, t % 2, LO, :, :], u.bank[:, :].rearrange("p (c l) -> p c l", c=CT),
                                    x2T[:, t % 2, HI, :, :].bitcast(F32), ALU.subtract).then_inc(x2T_ready, 1)

                def bn1(n):
                    if last or n >= NN:
                        return
                    wait_stage(dve, i, 1, n)
                    st(0, n, stage[0:rows_of(n), n % 3, :], rows_of(n))

                def n1(n):
                    if last or n >= NN:
                        return
                    norm1(i * NN + NN, n, T("x", n - 3).full_at if n >= 3 else None)

                def fin_out(t):
                    d = Dn("f", t)
                    dve.wait_ge(dense_full, d.full_at)
                    dve.wait_ge(fb_added, i * LT + t + 1)
                    v.tensor_tensor(v_x1[:, t, :], d.bank[:, :], v_x1[:, t, :], ALU.add).then_inc(out_ready, 1)

                res1(0)
                res1(1), norm2(0)
                res1(2), norm2(1), bn1(0)
                res1(3), n1(0), bn1(1)
                res1(4), n1(1), bn1(2)
                res1(5), n1(2), bn1(3)
                x2_lo(0), res1(6), norm2(2)
                x2_lo(1), res1(7), norm2(3)
                for t in range(LT):
                    fin_out(t)
                    if t + 2 < LT:
                        x2_lo(t + 2)
                    if not last:
                        xT_lo(T("x", t), t, i * NN + NN)
                    if t + 4 < LT:
                        norm2(t + 4)
                    n1(t + 3)
                    bn1(t + 4)
                if not last:
                    xT_lo(T("x", LT), LT, i * NN + NN)

            with dve.Fori(0, LAST) as i:
                batch(i, False)
            batch(LAST, True)


_INS = ["x", "wq", "bq", "wk", "bk", "wv", "bv", "wo", "bo", "idx_k", "wfr", "wfi", "fbias", "c32", "c16", "trig"]


def kernel(L0_attn_x, L0_attn_Wq, L0_attn_bq, L0_attn_Wk, L0_attn_bk, L0_attn_Wv, L0_attn_bv, L0_attn_Wo,
           L0_attn_bo, L0_attn_idx_k, L0_ffn_w_freq_real, L0_ffn_w_freq_imag, L0_ffn_bias):
    import concourse.bacc as bacc
    from concourse.bass_utils import run_bass_kernel_spmd

    x = np.ascontiguousarray(L0_attn_x)
    idx_k = np.ascontiguousarray(L0_attn_idx_k)
    c32, c16, trig = constants(*shapes_of(x, idx_k))
    turned = [np.ascontiguousarray(np.asarray(w).T) for w in (L0_attn_Wq, L0_attn_Wk, L0_attn_Wv, L0_attn_Wo)]
    bq, bk, bv = [column_tiles(b) for b in (L0_attn_bq, L0_attn_bk, L0_attn_bv)]
    values = [x, turned[0], bq, turned[1], bk, turned[2], bv, turned[3], L0_attn_bo, idx_k,
              L0_ffn_w_freq_real, L0_ffn_w_freq_imag, L0_ffn_bias, c32, c16, trig]
    nc = bacc.Bacc("TRN2", target_bir_lowering=False, num_devices=1)
    arrays, args = {}, []
    for name, a in zip(_INS, values):
        a = np.ascontiguousarray(a)
        arrays[f"in_{name}"] = a
        args.append(nc.dram_tensor(f"in_{name}", a.shape, mybir.dt.from_np(a.dtype), kind="ExternalInput").ap())
    out = nc.dram_tensor("out", x.shape, F32, kind="ExternalOutput").ap()
    build(nc, *args, out)
    r = run_bass_kernel_spmd(nc, [arrays], core_ids=[0])
    return r.results[0]["out"]
```

```python
from contextlib import ExitStack

import numpy as np

import concourse.bass as bass
from concourse import mybir

ALU = mybir.AluOpType
ACT = mybir.ActivationFunctionType
AX_X = mybir.AxisListType.X
AX_XY = mybir.AxisListType.XY
F32 = mybir.dt.float32
F32R = mybir.dt.float32r
F16 = mybir.dt.float16
U32 = mybir.dt.uint32
I32 = mybir.dt.int32

P = 128
EPS = 1e-5
HI, LO = 0, 1
MARK = 2048.0

C_IDENT, C_HEAD, C_QHALF, C_DMASK, C_HROW, C_IDX0 = 0, 128, 132, 136, 200, 208
C_END = 216


def shapes_of(x, idx_k):
    B, L, D = x.shape
    H = 16
    U = idx_k.shape[0] if len(idx_k.shape) == 1 else idx_k.shape[0] * idx_k.shape[1] // B
    return B, L, D, H, D // H, U


def constants(B, L, D, H, DK, U):
    HU = 2 * U
    BASE = (HU + 31) // 32 * 32
    c32 = np.zeros((P, C_END), np.float32)
    c32[:, C_IDENT:C_IDENT + P] = np.eye(P)
    for h in range(4):
        c32[h * DK:(h + 1) * DK, C_HEAD + h] = 1.0
    for a in range(2):
        c32[a * U:(a + 1) * U, [C_QHALF + a, C_QHALF + 2 + a]] = 1.0
        c32[a * U:(a + 1) * U, C_DMASK + a * DK:C_DMASK + (a + 1) * DK] = 1.0
    c32[BASE, C_DMASK:C_DMASK + 2 * DK] = 1.0
    for p in range(H // 2):
        c32[:HU, C_HROW + p] = 2 * p + (np.arange(HU) >= U)
    c32[:, C_IDX0:C_IDX0 + H // 2] = -1.0
    c32[BASE, C_IDX0:C_IDX0 + H // 2] = MARK
    c16 = np.zeros((P, L + H * U + 2), np.float16)
    c16[:, :L] = np.arange(L)
    c16[BASE, :L] = MARK
    for h in range(H):
        c16[h, L + h * U:L + (h + 1) * U] = 1.0
    c16[:, L + H * U:] = 1.0
    k = np.arange(D)
    ang = 2.0 * np.pi * ((k[:, None] * k[None, :D // 2 + 2]) % D) / D
    trig = np.stack([np.cos(ang), np.sin(ang)]).astype(np.float32)
    SR, NS = sample_tiles(B, U)
    first = (np.arange(B * U) // U * L).astype(np.float32)
    base = np.zeros((P, NS), np.float32)
    base[:SR] = first.reshape(NS, SR).T
    return c32, c16, trig, base


def sample_tiles(B, U):
    SR = max(r for r in range(1, P + 1) if (B * U) % r == 0)
    return SR, B * U // SR


def sample_positions(idx_k, B):
    SR, NS = sample_tiles(B, idx_k.shape[0])
    return np.ascontiguousarray(np.tile(np.asarray(idx_k), B).reshape(NS, SR).T)


def column_tiles(bias):
    return np.ascontiguousarray(np.asarray(bias).reshape(-1, P).T)


def build(nc, x, wq, bq, wk, bk, wv, bv, wo, bo, wfr, wfi, fbias, c32, c16, trig, sbase, spos, out):
    B, L, D, H, DK, U = shapes_of(x, spos)
    LT = L // P
    CT = D // P
    NP_ = H // 2
    HU = 2 * U
    BASE = (HU + 31) // 32 * 32
    KR = BASE + 1
    SW = 4 * U + 4
    SR, NS = sample_tiles(B, U)
    FH = D // 2 + 1
    SCALE = float(DK) ** -0.5
    LAST = B - 1

    q_rows = nc.dram_tensor("q_rows", (L * H, DK), F32, kind="Internal").ap()
    q_by_row = q_rows.rearrange("(t p h) d -> p t (h d)", p=P, h=H)
    x_rows = x.rearrange("b l d -> (b l) d")
    k_samples = nc.dram_tensor("k_samples", (P, CT, B * U), F32, kind="Internal").ap()

    ctx = ExitStack()
    with ctx:
        def sb(name, shape, dt):
            return ctx.enter_context(nc.sbuf_tensor(name, shape, dt))

        def early(name, shape, dt):
            with nc.sbuf_tensor(name, shape, dt) as t:
                return t

        def sem(name):
            return ctx.enter_context(nc.semaphore(name))

        W = {n: sb(f"w_{n}", [P, 2, CT, D], F32R) for n in ("q", "k", "v", "o")}
        fin = early("fourier_w", [P, 2, CT, D], F32)
        W["g"] = sb("w_g", [P, 2, CT, D], F32R)
        xT = sb("xT", [P, 2, CT, L], F32R)
        scr = early("scratch", [P, 4 * L], F32)
        kp = sb("k_pairs", [P, 4, L], F32R)
        v_x1 = sb("v_x1", [P, LT, D], F32)
        pre = early("before_loop", [P, 4 * L], F32)
        TRI = 2 * CT * (FH + 1)
        tri = pre[:, 0:TRI].rearrange("p (t c n) -> p t c n", t=2, c=CT)
        K_AT = (TRI, TRI + D)
        pre_r = early("before_loop_r", [P, 4 * L], F32R)
        XS = TRI + 2 * D
        xs0 = pre_r[:, XS:XS + 2 * CT * SR].rearrange("p (a c r) -> p a c r", a=2, c=CT)
        q_phase = early("q_phase", [P, 4 * L], F32)
        q_e = q_phase[:, 0:2048].rearrange("p (s n) -> p s n", s=4)
        kbd = q_phase[:, 2048:2048 + CT * SW].rearrange("p (c k) -> p c k", c=CT)
        oh = sb("onehot", [P, 4, L], F32R)
        stage = sb("stage", [P, 4, D], F32)
        xn1 = sb("xn1", [P, 2, D], F32)
        xn2 = sb("xn2", [P, 2, D], F32)
        prob = early("prob", [P, 2, L], F32)
        x2T = sb("x2T", [P, 2, 2, CT, P], F32R)
        pT = sb("pT", [P, 2, LT, BASE + 2], F32)
        cst = sb("cst", [P, C_END], F32)
        cst16 = sb("cst16", [P, L + H * U + 2], F16)
        mval = sb("mval", [P, LT, H], F32)
        mT = prob[0:H, 0, :]
        top_v = sb("top_v", [H, 48], F32)
        top_i = sb("top_i", [H, 48], U32)
        top_f = sb("top_f", [H, 48], F32)
        rsel = sb("rsel", [H, H, U], F16)
        idxc = sb("idxc", [P, NP_], F32)
        qidx = sb("qidx", [P, NP_], U32)
        qg = sb("qg", [P, NP_, DK], F32)
        qx = sb("qx", [P, 4, P], F32)
        qtT = sb("qtT", [P, 4, 2, HU], F32R)
        ks = sb("ks", [P, CT, U], F32)
        ksum = sb("ksum", [P, CT, 4], F32)
        dtmp = sb("dtmp", [P, 2, 2 * DK], F32)
        xs1 = early("xsT1", [P, 2, CT, SR], F32R)
        delta = sb("delta", [P, 2, 2, 2, P], F32R)
        bo_b = sb("bo_b", [P, D], F32)
        fb_b = sb("fb_b", [P, D], F32)
        bq_c = sb("bq_c", [P, CT], F32)
        bk_c = sb("bk_c", [P, CT], F32)
        bv_c = sb("bv_c", [P, CT], F32)
        sidx = sb("sidx", [P, NS], I32)
        sbs = sb("sbs", [P, NS], F32)
        soff = sb("soff", [P, 5, NS], F32)
        soffu = sb("soffu", [P, NS], U32)
        mhalf = sb("mhalf", [P, 1], F32)
        bst = sb("bst", [P, 2, LT, 6], F32)
        mv = [sb(f"mv{k}", [P, LT, 2], F32) for k in range(2)]
        vep = [sb(f"vep{k}", [P, LT], F32) for k in range(2)]
        rstd = [sb(f"rstd{k}", [P, LT], F32) for k in range(2)]
        nmr = [sb(f"nmr{k}", [P, LT], F32) for k in range(2)]
        negmax = sb("negmax", [P, 2, 2], F32)
        psum_ = sb("psum_", [P, 2, 2], F32)

        dense = [ctx.enter_context(nc.psum_tensor(f"dense{k}", [P, 512], F32)) for k in range(2)]
        turn = [ctx.enter_context(nc.psum_tensor(f"turn{k}", [P, 512], F32)) for k in range(2)]
        score = ctx.enter_context(nc.psum_tensor("score", [P, 4, 512], F32))

        ident = cst[:, C_IDENT:C_IDENT + P]
        kst = scr[:, 776:776 + CT * B * U].rearrange("p (c r) -> p c r", c=CT)

        consts_in = sem("consts_in")
        positions_in = sem("positions_in")
        fourier_in = [sem(f"fourier_in{k}") for k in range(6)]
        weight_in = sem("weight_in")
        weight_hi = sem("weight_hi")
        weight_lo = sem("weight_lo")
        bias_in = sem("bias_in")
        g_full = sem("g_full")
        g_copied = sem("g_copied")
        g_hi = sem("g_hi")
        g_lo = sem("g_lo")
        bv_spread = sem("bv_spread")
        bo_full = sem("bo_full")
        bo_ready = sem("bo_ready")
        cleared = sem("cleared")
        soff_step = sem("soff_step")
        soff_ready = sem("soff_ready")
        xs_hi = sem("xs_hi")
        xs_ready = sem("xs_ready")
        ksr_ready = sem("ksr_ready")
        kst_ready = sem("kst_ready")
        kst_stored = sem("kst_stored")
        ks_in = sem("ks_in")
        g_joined = sem("g_joined")
        sampled_in = [sem(f"sampled_in{k}") for k in range(4)]
        stage_in = [sem(f"stage_in{k}") for k in range(4)]
        mean_ready = [sem(f"mean_ready{k}") for k in range(2)]
        eps_added = sem("eps_added")
        powered = sem("powered")
        rstd_ready = [sem(f"rstd_ready{k}") for k in range(2)]
        norm_done = [sem(f"norm_done{k}") for k in range(2)]
        turn_full = sem("turn_full")
        dense_full = sem("dense_full")
        xT_hi = sem("xT_hi")
        xT_ready = sem("xT_ready")
        x2T_hi = sem("x2T_hi")
        x2T_ready = sem("x2T_ready")
        kbd_step = sem("kbd_step")
        kbd_ready = sem("kbd_ready")
        qT_ready = sem("qT_ready")
        qrow_ready = sem("qrow_ready")
        q_stored = [sem(f"q_stored{k}") for k in range(2)]
        m_full = sem("m_full")
        m_max = sem("m_max")
        m_free = sem("m_free")
        mT_full = sem("mT_full")
        top_max = sem("top_max")
        stats_done = sem("stats_done")
        top_found = sem("top_found")
        top_struck = sem("top_struck")
        top_float = sem("top_float")
        rsel_ready = sem("rsel_ready")
        idx_full = sem("idx_full")
        idxc_ready = sem("idxc_ready")
        qidx_ready = sem("qidx_ready")
        q_gathered = [sem(f"q_gathered{k}") for k in range(NP_)]
        qx_ready = sem("qx_ready")
        qx_pool = sem("qx_pool")
        qtT_hi = sem("qtT_hi")
        qtT_ready = sem("qtT_ready")
        k_full = sem("k_full")
        k_hi = sem("k_hi")
        k_ready = sem("k_ready")
        v_ready = sem("v_ready")
        s_full = sem("s_full")
        o_full = sem("o_full")
        s_max = sem("s_max")
        negmax_ready = sem("negmax_ready")
        exp_done = sem("exp_done")
        recip_done = sem("recip_done")
        prob_ready = sem("prob_ready")
        pT_ready = sem("pT_ready")
        dtmp_ready = sem("dtmp_ready")
        delta_hi = sem("delta_hi")
        delta_ready = sem("delta_ready")
        oh_ready = sem("oh_ready")
        ctx_hi = sem("ctx_hi")
        ctx_ready = sem("ctx_ready")
        xres_in = [sem(f"xres_in{k}") for k in range(LT)]
        bo_added = sem("bo_added")
        x1_ready = sem("x1_ready")
        fb_added = sem("fb_added")
        out_ready = sem("out_ready")
        out_stored = sem("out_stored")

        def turn_order(last):
            o = [("q", u) for u in range(8)] + [("qt", 0), ("qt", 1), ("qt", 2)]
            for p in range(NP_):
                if p + 3 < NP_:
                    o.append(("qt", p + 3))
                o += [("p", p, 0), ("p", p, 1)]
            o += [("x2", 0), ("x2", 1)]
            for t in range(LT):
                if t + 2 < LT:
                    o.append(("x2", t + 2))
                if not last:
                    o.append(("x", t))
            return o

        SCATTER_AT = {4: 0, 5: 1, 7: 2}

        def dense_order():
            o = [("q", u) for u in range(8)] + [("v", t) for t in range(LT)] + [("k", 2), ("k", 3)]
            for p in range(NP_):
                if p < 4:
                    o.append(("k", 4 + p))
                if p >= 1:
                    o.append(("pv", p - 1))
                if p in SCATTER_AT:
                    o += [("sc", SCATTER_AT[p], h) for h in range(2)]
            o += [("pv", NP_ - 1), ("sc", 3, 0), ("sc", 3, 1)]
            o += [("o", t) for t in range(4, LT)] + [("f", t) for t in range(LT)]
            return o

        MIDDLE, AFTER = [[] for _ in range(8)], [[] for _ in range(8)]
        for k in range(0, NS, 2):
            two = range(k, min(k + 2, NS))
            at = [min(k // 2 + 1 + n, 7) for n in range(3)]
            AFTER[at[0]] += [("s", j) for j in two]
            AFTER[at[1]] = [("km", j) for j in two] + AFTER[at[1]]
            (MIDDLE if k == NS - 2 else AFTER)[at[2]][:0] = [("st", j) for j in two]
            for part in AFTER:
                part.sort(key=lambda item: ("st", "km", "s").index(item[0]))
        for n in range(LT):
            (AFTER[4], AFTER[5], MIDDLE[6], AFTER[6])[n * 4 // LT].append(("x", n))
        FIRST = [k for both in zip(MIDDLE, AFTER) for part in both for k in part]
        FIRST_TURNS = [k for k in FIRST if k[0] != "km"]
        FT = len(FIRST_TURNS)
        assert NS % 2 == 0 and FT % 2 == 0 and FIRST_TURNS[-2:] == [("x", LT - 2), ("x", LT - 1)]
        TURNS = {last: {k: n for n, k in enumerate(turn_order(last))} for last in (False, True)}
        DENSES = {k: n for n, k in enumerate(dense_order())}
        TPI, DPI = len(TURNS[False]), len(DENSES)
        assert TPI % 2 == 0 and DPI % 2 == 0

        def taken_of(RING, key, i):
            kind, n = key[0], (key[1] if len(key) > 1 else 0)
            return {
                ("d", "q"): lambda: (qT_ready, i * 8 + n + 1),
                ("d", "v"): lambda: (v_ready, i * LT + n + 1),
                ("d", "k"): lambda: (k_ready, i * 8 + n + 1),
                ("d", "pv"): lambda: (dtmp_ready, i * NP_ + n + 1),
                ("d", "sc"): lambda: (ctx_ready, i * 8 + 2 * n + key[2] + 1),
                ("d", "o"): lambda: (x1_ready, i * LT + n + 1),
                ("d", "f"): lambda: (out_ready, i * LT + n + 3),
                ("t", "s"): lambda: (xs_ready, n + 1),
                ("t", "st"): lambda: (kst_ready, n + 1),
                ("d", "km"): lambda: (ksr_ready, n + 1),
                ("t", "q"): lambda: (qrow_ready, i * 8 + n + 1),
                ("t", "qt"): lambda: (qtT_ready, i * NP_ + n + 1),
                ("t", "p"): lambda: (pT_ready, i * 2 * NP_ + 2 * n + key[2] + 1),
                ("t", "x2"): lambda: (x2T_ready, i * LT + n + 1),
                ("t", "x"): lambda: (xT_ready, i * LT + LT + n + 1),
            }[RING, kind]()

        class Use:
            def __init__(self, bank, free, full, full_at):
                self.bank, self.free, self.full, self.full_at = bank, free, full, full_at

        def turn_use(key, i, last):
            n = TURNS[last][key]
            names = list(TURNS[last])
            free = taken_of("t", names[n - 2], i) if n >= 2 else (xT_ready, i * LT + LT - 1 + n)
            return Use(turn[(FT + n) % 2], free, turn_full, i * TPI + FT + n + 1)

        def first_turn(*key):
            n = FIRST_TURNS.index(key)
            prev = FIRST_TURNS[n - 2] if n >= 2 else None
            free = taken_of("t", prev, -1 if prev[0] == "x" else 0) if prev else None
            return Use(turn[n % 2], free, turn_full, n + 1)

        def first_dense(k):
            return Use(dense[k % 2], taken_of("d", ("km", k - 2), 0) if k >= 2 else None, dense_full, k + 1)

        def dense_use(key, i):
            n = DENSES[key]
            free = taken_of("d", list(DENSES)[n - 2], i) if n >= 2 else (out_ready, i * LT + n + 1)
            return Use(dense[n % 2], free, dense_full, i * DPI + NS + n + 1)

        def spread(eng, p):
            return eng.tensor_tensor(qx[0:HU, p % 4, :].rearrange("r (x d) -> r x d", d=DK),
                                     qg[0:HU, p, :].unsqueeze(1).broadcast_to([HU, 4, DK]),
                                     cst[0:HU, C_QHALF:C_QHALF + 4].unsqueeze(2).broadcast_to([HU, 4, DK]), ALU.mult)

        def wait_keys(eng, n, i):
            if n < 2:
                eng.wait_ge(k_full, i * 2 + n + 1)
                return score[:, n, :]
            u = dense_use(("k", n), i)
            eng.wait_ge(dense_full, u.full_at)
            return u.bank[:, :]

        def wait_stage(eng, i, b, n):
            eng.wait_ge(stage_in[n % 4], 32 * i + 32 * b + 16 * (n // 4 + 1))

        block = ctx.enter_context(nc.Block())

        @block.sync
        def _(sp):
            sp.sem_inc(out_stored, 16)
            sp.dma_start(sidx[0:SR, :], spos).then_inc(positions_in, 16)
            sp.dma_start(sbs[:, :], sbase).then_inc(positions_in, 16)
            one, rest = slice(0, P), slice(P, D)
            for k, (src, dst) in enumerate(((trig[0], tri[:, 0]), (wfr[:, one], fin[:, 0, :, one]),
                                            (wfi[:, one], fin[:, 1, :, one]), (trig[1], tri[:, 1]),
                                            (wfr[:, rest], fin[:, 0, :, rest]), (wfi[:, rest], fin[:, 1, :, rest]))):
                sp.dma_start(dst, src.rearrange("(c p) n -> p c n", p=P)).then_inc(fourier_in[k], 16)
            sp.dma_start(cst[:, :], c32).then_inc(consts_in, 16)

            def weight(n, src):
                if n:
                    sp.wait_ge(weight_lo, n)
                sp.dma_start(prob[:, :, :].rearrange("p a (b n) -> p (a b) n", n=D),
                             src.rearrange("(c p) n -> p c n", p=P)).then_inc(weight_in, 16)

            weight(0, wk)
            for src, dst in ((bq, bq_c), (bk, bk_c), (bv, bv_c)):
                sp.dma_start(dst[:, :], src).then_inc(bias_in, 16)
            for src, dst in ((bo, bo_b), (fbias, fb_b)):
                sp.dma_start(dst[:, :], src.partition_broadcast(P)).then_inc(bias_in, 16)
            sp.dma_start(cst16[:, :], c16).then_inc(consts_in, 16)
            weight(1, wq)

            def first_tile(n):
                sp.wait_ge(norm_done[0], NS + n - 3 if n >= 4 else (NS - 1 - (NS - 1 - n) % 4) + 1)
                sp.dma_start(stage[:, n % 4, :], x[0, n * P:(n + 1) * P, :]).then_inc(stage_in[n % 4], 16)

            def keep(k):
                sp.wait_ge(kst_ready, k + 1)
                cols = slice(k * SR, (k + 1) * SR)
                sp.dma_start(k_samples[:, :, cols], kst[:, :, cols]).then_inc(kst_stored, 16)

            weight(2, wv)
            for n in range(6):
                first_tile(n)
            weight(3, wo)
            first_tile(6), first_tile(7)
            for k in range(NS):
                keep(k)
            sp.wait_ge(kst_stored, 16 * NS)
            sp.dma_start(ks[:, :, :], k_samples[:, :, 0:U]).then_inc(ks_in, 16)

            def batch(i, last):
                def next_tile(n):
                    if not last and n < LT:
                        sp.wait_ge(norm_done[0], i * LT + NS + LT + n - 3)
                        sp.dma_start(stage[:, n % 4, :], x[i + 1, n * P:(n + 1) * P, :]).then_inc(stage_in[n % 4], 16)

                for n in range(4):
                    next_tile(n)
                if not last:
                    sp.wait_ge(kbd_ready, i + 1)
                    sp.dma_start(ks[:, :, :], k_samples[:, :, bass.ds(i * U + U, U)]).then_inc(ks_in, 16)
                for u in range(8):
                    g, half = u // 2, u % 2
                    sp.wait_ge(qrow_ready, i * 8 + u + 1)
                    sp.dma_start(q_by_row[:, half * 4:half * 4 + 4, g * P:(g + 1) * P],
                                 q_e[:, 2 + u % 2, :].rearrange("p (t d) -> p t d", t=4)).then_inc(q_stored[u % 2], 16)

                sp.wait_ge(dense_full, dense_use(("pv", NP_ - 1), i).full_at)
                for t in range(LT):
                    sp.dma_start(v_x1[:, t, :], x[i, t * P:(t + 1) * P, :]).then_inc(xres_in[t], 16)
                for n in range(4, 6):
                    next_tile(n)
                for t in range(LT):
                    sp.wait_ge(out_ready, i * LT + t + 3)
                    sp.dma_start(out[i, t * P:(t + 1) * P, :], v_x1[:, t, :]).then_inc(out_stored, 16)
                    next_tile(t + 6)

            with sp.Fori(0, LAST) as i:
                batch(i, False)
            batch(LAST, True)
            sp.wait_ge(out_stored, 16 * LT * B + 16)
            for k in range(2):
                sp.wait_ge(q_stored[k], 16 * 4 * B)

        def standing(eng):
            eng.nop(nofuse=True)

        @block.gpsimd
        def _(pool):
            pool.memset(mhalf[:, :], -0.5).then_inc(cleared, 1)
            pool.memset(pT[:, :, :, :], 0.0).then_inc(cleared, 1)
            pool.wait_ge(cleared, 2)
            pool.memset(pT[:, :, :, BASE:BASE + 1], 1.0 / L).then_inc(cleared, 1)

            def sample_rows(k):
                if k >= 4:
                    pool.wait_ge(norm_done[0], k - 3)
                    standing(pool)
                pool.indirect_dma_start(stage[0:SR, k % 4, :], None, x_rows[:, :],
                                        bass.IndirectOffsetOnAxis(ap=soffu[0:SR, k:k + 1], axis=0)).then_inc(sampled_in[k % 4], 16)

            def power(which, count, nth, n, rows):
                pool.wait_ge(mean_ready[which], count + 1)
                standing(pool)
                pool.tensor_scalar(vep[which][0:rows, n:n + 1], mv[which][0:rows, n, 1:2], EPS, 1.0,
                                   ALU.add, ALU.mult).then_inc(eps_added, 1)
                pool.wait_ge(eps_added, nth + 1)
                pool.tensor_tensor(rstd[which][0:rows, n:n + 1], vep[which][0:rows, n:n + 1],
                                   mhalf[0:rows, :], ALU.pow).then_inc(powered, 1)
                pool.wait_ge(powered, nth + 1)
                standing(pool)
                pool.tensor_scalar(nmr[which][0:rows, n:n + 1], mv[which][0:rows, n, 0:1], -1.0,
                                   rstd[which][0:rows, n:n + 1], ALU.mult, ALU.mult).then_inc(rstd_ready[which], 1)

            pool.wait_ge(soff_ready, 1)
            standing(pool)
            for k in range(min(4, NS)):
                sample_rows(k)
            for k in range(NS):
                power(0, k, k, k % LT, SR)
                if k + 4 < NS:
                    sample_rows(k + 4)
            for n in range(LT):
                power(0, NS + n, NS + n, n, P)
            pool.wait_ge(dense_full, NS)
            pool.memset(delta[:, :, :, :, :].bitcast(F32), 0.0).then_inc(cleared, 1)
            PER = 2 * LT

            def batch(i, last):
                tiles = [0]

                def rstd1(n):
                    if not last and n < LT:
                        power(0, i * LT + NS + LT + n, i * PER + NS + LT + tiles[0], n, P)
                        tiles[0] += 1

                def rstd2(t):
                    power(1, i * LT + t, i * PER + NS + LT + tiles[0], t, P)
                    tiles[0] += 1

                def add_fb(t):
                    pool.wait_ge(norm_done[1], i * LT + t + 1)
                    pool.tensor_tensor(v_x1[:, t, :], v_x1[:, t, :], fb_b[:, :], ALU.add).then_inc(fb_added, 1)

                for n in range(4):
                    rstd1(n)
                for s in range(2):
                    pool.wait_ge(q_stored[s], i * 64 + 64)
                pool.wait_ge(qidx_ready, i + 1)
                standing(pool)
                for p in range(NP_):
                    pool.indirect_dma_start(qg[0:HU, p, :], None, q_rows[:, :],
                                            bass.IndirectOffsetOnAxis(ap=qidx[0:HU, p:p + 1], axis=0)
                                            ).then_inc(q_gathered[p], 16)

                def onehot(p):
                    if p >= 4 and p % 2 == 0:
                        pool.wait_ge(dense_full, dense_use(("sc", p // 2 - 2, 1), i).full_at)
                        standing(pool)
                    pool.tensor_scalar(oh[0:KR, p % 4, :], cst16[0:KR, 0:L], idxc[0:KR, p:p + 1], None,
                                       ALU.is_equal).then_inc(oh_ready, 1)

                for p in range(NP_):
                    if p < 4:
                        pool.wait_ge(q_gathered[p + 4], i * 16 + 16)
                        pool.wait_ge(turn_full, turn_use(("qt", p), i, last).full_at)
                        standing(pool)
                        spread(pool, p + 4).then_inc(qx_pool, 1)
                    onehot(p)
                pool.wait_ge(bo_ready, 1)

                def add_bo(t):
                    pool.wait_ge(xres_in[t], i * 16 + 16)
                    pool.tensor_tensor(v_x1[:, t, :], v_x1[:, t, :], bo_b[:, :], ALU.add).then_inc(bo_added, 1)

                add_bo(0), add_bo(1), add_bo(2), rstd2(0), add_bo(3), rstd2(1), add_bo(4), rstd2(2)
                add_bo(5), add_bo(6), rstd2(3), add_bo(7), rstd2(4)
                add_fb(0), rstd2(5), add_fb(1), rstd2(6), rstd2(7), add_fb(2), add_fb(3)
                for t in range(LT):
                    rstd1(t + 4)
                    if t + 4 < LT:
                        add_fb(t + 4)

            with pool.Fori(0, LAST) as i:
                batch(i, False)
            batch(LAST, True)

        @block.scalar
        def _(act):
            def wstage():
                return prob[:, :, :].rearrange("p a (b n) -> p (a b) n", n=D)

            def weight(n):
                act.wait_ge(weight_in, 16 * (n + 1))
                nc.scalar.activation(W["kqvo"[n]][:, HI], wstage(), ACT.Copy).then_inc(weight_hi, 1)

            def hi_of_turn(u, dst, done):
                act.wait_ge(turn_full, u.full_at)
                nc.scalar.activation(dst, u.bank[:, :].rearrange("p (c l) -> p c l", c=CT)[:, :, 0:dst.shape[-1]],
                                     ACT.Copy).then_inc(done, 1)

            def normal(which, count, n, src, dst, rows):
                act.wait_ge(rstd_ready[which], count + 1)
                nc.scalar.activation(dst, src, ACT.Identity, scale=rstd[which][0:rows, n:n + 1],
                                     bias=nmr[which][0:rows, n:n + 1]).then_inc(norm_done[which], 1)

            def xT_dst(n):
                return xT[:, HI, :, n * P:(n + 1) * P]

            def first_norm(m):
                s_, n = (True, m) if m < NS else (False, m - NS)
                if m >= 2:
                    key = ("s", m - 2) if m - 2 < NS else ("x", m - 2 - NS)
                    act.wait_ge(turn_full, first_turn(*key).full_at)
                rows = SR if s_ else P
                normal(0, m, n % LT, stage[0:rows, n % 4, :], xn1[0:rows, n % 2, :], rows)


            def first_work(key):
                kind, k = key
                if kind == "s":
                    if k >= 2:
                        act.wait_ge(dense_full, k - 1)
                    hi_of_turn(first_turn(*key), (xs0, xs1)[k % 2][:, HI], xs_hi)
                    first_norm(k + 2)
                elif kind == "km":
                    act.wait_ge(dense_full, k + 1)
                    if k >= 2:
                        act.wait_ge(turn_full, first_turn("st", k - 2).full_at)
                    nc.scalar.activation(pre[0:SR, K_AT[k % 2]:K_AT[k % 2] + D], dense[k % 2][0:SR, :],
                                         ACT.Copy).then_inc(ksr_ready, 1)
                elif kind == "st":
                    u = first_turn(*key)
                    act.wait_ge(turn_full, u.full_at)
                    for g in range(CT):
                        m = nc.scalar.activation(kst[:, g, k * SR:(k + 1) * SR], u.bank[:, g * P:g * P + SR], ACT.Identity,
                                                 bias=bk_c[:, g:g + 1])
                    m.then_inc(kst_ready, 1)
                else:
                    hi_of_turn(first_turn(*key), xT_dst(k), xT_hi)
                    if NS + k + 2 < NS + LT:
                        first_norm(NS + k + 2)

            for j in range(8):
                for key in MIDDLE[j]:
                    first_work(key)
                for h in range(2 if j < 4 else 1):
                    act.wait_ge(g_full, 4 * j + 2 * h + 2 if j < 4 else 16 + 2 * (j - 4) + 2)
                    if j and h == 0:
                        act.wait_ge(g_joined, j)
                    a0 = (0, 258)[h] if j < 4 else 516
                    bank = 2 * h + 1 if j < 4 else 2 * (j % 2) + 1
                    nc.scalar.activation(scr[:, a0:a0 + FH], score[:, bank, 0:FH], ACT.Copy,
                                         scale=1.0 if j < 4 else 1.0 / D).then_inc(g_copied, 1)
                if j >= 4:
                    act.wait_ge(g_joined, j + 1)
                    nc.scalar.activation(W["g"][:, HI, j - 4, :], scr[:, 0:D], ACT.Copy).then_inc(g_hi, 1)
                if j == 0:
                    first_norm(0), first_norm(1)
                    act.wait_ge(bias_in, 80)
                if j < 2:
                    weight(j)
                if j == 3:
                    weight(2)
                if j == 6:
                    weight(3)
                for key in AFTER[j]:
                    first_work(key)

            def batch(i, last):
                T = lambda *k: turn_use(k, i, last)
                Dn = lambda *k: dense_use(k, i)

                def q_out(n):
                    d = Dn("q", n)
                    act.wait_ge(dense_full, d.full_at)
                    if n >= 2:
                        act.wait_ge(turn_full, T("q", n - 2).full_at)
                    nc.scalar.activation(q_e[:, n % 2, :], d.bank[:, :], ACT.Identity,
                                         bias=bq_c[:, n // 2:n // 2 + 1]).then_inc(qT_ready, 1)

                def qrow_out(n):
                    d = T("q", n)
                    act.wait_ge(turn_full, d.full_at)
                    if n >= 2:
                        act.wait_ge(q_stored[n % 2], i * 64 + 16 * (n // 2))
                    nc.scalar.activation(q_e[:, 2 + n % 2, :], d.bank[:, :], ACT.Copy).then_inc(qrow_ready, 1)

                q_out(0)
                for n in range(1, 8):
                    q_out(n)
                    qrow_out(n - 1)
                qrow_out(7)

                def v_out(t):
                    d = Dn("v", t)
                    act.wait_ge(dense_full, d.full_at)
                    if t == 0:
                        act.wait_ge(out_stored, i * 16 * LT + 16)
                    nc.scalar.activation(v_x1[:, t, :], d.bank[:, :], ACT.Copy).then_inc(v_ready, 1)

                for t in range(LT):
                    v_out(t)

                def k_out(n):
                    g, half = n // 2, n % 2
                    bank = wait_keys(act, n, i)
                    for e in range(2):
                        r_ = slice(64 * e, 64 * e + 64)
                        m = nc.scalar.activation(kp[r_, 2 * (g % 2) + e, half * 512:half * 512 + 512],
                                                 bank[r_, :], ACT.Identity, bias=bk_c[r_, g:g + 1])
                    m.then_inc(k_hi, 1)

                def qt_out(p):
                    u = T("qt", p)
                    act.wait_ge(turn_full, u.full_at)
                    if p >= 4:
                        act.wait_ge(s_full, i * NP_ + p - 3)
                    nc.scalar.activation(qtT[:, p % 4, HI, :], u.bank[:, 0:HU], ACT.Copy).then_inc(qtT_hi, 1)

                def exps(p):
                    act.wait_ge(negmax_ready, i * NP_ + p + 1)
                    if p >= 2:
                        act.wait_ge(turn_full, T("p", p - 2, 1).full_at)
                    nc.scalar.activation(prob[0:HU, p % 2, :], score[0:HU, 2 * (p % 2):2 * (p % 2) + 2, :], ACT.Exp,
                                         bias=negmax[0:HU, p % 2, 1:2], scale=SCALE,
                                         accum_out=psum_[0:HU, p % 2, 0:1]).then_inc(exp_done, 1)

                def pT_out(p):
                    for h in range(2):
                        u = T("p", p, h)
                        act.wait_ge(turn_full, u.full_at)
                        nc.scalar.activation(pT[:, p % 2, 4 * h:4 * h + 4, 0:HU],
                                             u.bank[:, :].rearrange("p (t r) -> p t r", t=4)[:, :, 0:HU],
                                             ACT.Copy).then_inc(pT_ready, 1)

                def sc_out(g):
                    for h in range(2):
                        d = Dn("sc", g, h)
                        act.wait_ge(dense_full, d.full_at)
                        nc.scalar.activation(xT[:, HI, g, h * 512:h * 512 + 512], d.bank[:, :],
                                             ACT.Copy).then_inc(ctx_hi, 1)

                def norm1(n):
                    if last or n >= LT:
                        return
                    if n >= 2:
                        act.wait_ge(turn_full, T("x", n - 2).full_at)
                    normal(0, i * LT + NS + LT + n, n, stage[:, n % 4, :], xn1[:, n % 2, :], P)

                for n in range(3):
                    k_out(n)
                qt_out(0)
                qt_out(1)
                k_out(3)
                qt_out(2)
                exps(0)
                for p in range(NP_):
                    if p + 3 < NP_:
                        qt_out(p + 3)
                    if 1 <= p < NP_ - 1:
                        exps(p + 1)
                    if p < 4:
                        k_out(4 + p)
                    if p in SCATTER_AT:
                        sc_out(SCATTER_AT[p])
                    pT_out(p)
                    if p == 0:
                        exps(1)
                    if p >= NP_ - 2:
                        norm1(p - NP_ + 2)
                sc_out(3)

                def x2_out(t):
                    hi_of_turn(T("x2", t), x2T[:, t % 2, HI, :, :], x2T_hi)

                def norm2(t):
                    if t >= LT:
                        return
                    if t >= 2:
                        act.wait_ge(turn_full, T("x2", t - 2).full_at)
                    normal(1, i * LT + t, t, v_x1[:, t, :], xn2[:, t % 2, :], P)

                norm2(0), norm2(1)
                x2_out(0), norm2(2)
                x2_out(1), norm2(3)
                for t in range(LT):
                    if t + 2 < LT:
                        x2_out(t + 2)
                    if not last:
                        hi_of_turn(T("x", t), xT_dst(t), xT_hi)
                    norm2(t + 4)
                    norm1(t + 2)

            act.wait_ge(cleared, 4)
            with act.Fori(0, LAST) as i:
                batch(i, False)
            batch(LAST, True)

        @block.tensor
        def _(pe):
            mm = nc.tensor.matmul

            def three_pass(dst, pairs, between=None):
                todo = [(l[a], r[b]) for l, r in pairs for a, b in ((HI, HI), (HI, LO), (LO, HI))]
                for n, (l, r) in enumerate(todo):
                    if between and n == len(todo) // 2:
                        between()
                    m = mm(dst, l, r, start=(n == 0), stop=(n == len(todo) - 1))
                return m

            def turn_tile(u, src, rows, ncol=CT):
                if u.free:
                    pe.wait_ge(*u.free)
                if rows < P:
                    standing(pe)
                for c in range(ncol):
                    m = nc.tensor.transpose(u.bank[:, c * P:c * P + rows], src[0:rows, c * P:(c + 1) * P],
                                            ident[0:rows, 0:rows])
                m.then_inc(turn_full, 1)

            def g_part(j):
                if j < 4:
                    for n, (w, t) in enumerate(((0, 0), (1, 1), (0, 1), (1, 0))):
                        if j == 0:
                            for k in ((0, 1), (2, 3), (), ())[n]:
                                pe.wait_ge(fourier_in[k], 16)
                        elif n == 0:
                            pe.wait_ge(g_joined, j)
                            if j == 1:
                                pe.wait_ge(fourier_in[4], 16)
                                pe.wait_ge(fourier_in[5], 16)
                        for c in range(CT):
                            m = mm(score[:, n, 0:FH], fin[:, w, c, j * P:(j + 1) * P], tri[:, t, c, 0:FH],
                                   start=(c == 0), stop=(c == CT - 1))
                        m.then_inc(g_full, 1)
                else:
                    n = j - 4
                    pe.wait_ge(g_joined, 4 if n < 2 else j - 1)
                    for t in range(2):
                        for key in MIDDLE[j] if t else ():
                            first_work(key)
                        for o in range(CT):
                            m = mm(score[:, 2 * (j % 2) + t, 0:FH], v_x1[:, 4 * t + o, n * P:(n + 1) * P],
                                   tri[:, t, o, 0:FH], start=(o == 0), stop=(o == CT - 1))
                        m.then_inc(g_full, 1)

            def first_work(key):
                kind, k = key
                if kind == "s":
                    pe.wait_ge(norm_done[0], k + 1)
                    turn_tile(first_turn(*key), xn1[:, k % 2, :], SR)
                elif kind == "km":
                    d = first_dense(k)
                    if d.free:
                        pe.wait_ge(*d.free)
                    if k == 0:
                        pe.wait_ge(weight_lo, 1)
                    pe.wait_ge(xs_ready, k + 1)
                    xs = (xs0, xs1)[k % 2]
                    three_pass(d.bank[0:SR, :], [([xs[:, a, c, :] for a in (HI, LO)],
                                                  [W["k"][:, a, c, :] for a in (HI, LO)]) for c in range(CT)]
                               ).then_inc(dense_full, 1)
                elif kind == "st":
                    pe.wait_ge(ksr_ready, k + 1)
                    turn_tile(first_turn(*key), pre[:, K_AT[k % 2]:K_AT[k % 2] + D], SR)
                else:
                    pe.wait_ge(norm_done[0], NS + k + 1)
                    turn_tile(first_turn(*key), xn1[:, k % 2, :], P)

            for j in range(8):
                g_part(j)
                if j == 0:
                    pe.wait_ge(consts_in, 32)
                for key in AFTER[j]:
                    first_work(key)
            pe.wait_ge(bv_spread, 1)
            pe.wait_ge(weight_in, 64)
            pe.wait_ge(g_joined, 7)
            for c in range(CT):
                m = mm(score[:, 0, :], xn2[:, 0, c * P:(c + 1) * P],
                       prob[:, c // 2, (c % 2) * 512:(c % 2) * 512 + 512], start=(c == 0), stop=(c == CT - 1))
            m.then_inc(bo_full, 1)

            def batch(i, last):
                T = lambda *k: turn_use(k, i, last)
                Dn = lambda *k: dense_use(k, i)

                def q_proj(n):
                    g, half = n // 2, n % 2
                    d = Dn("q", n)
                    pe.wait_ge(*d.free)
                    if n < 2:
                        pe.wait_ge(xT_ready, i * LT + 4 * (half + 1))
                    three_pass(d.bank[:, :],
                               [([W["q"][:, a, c, g * P:(g + 1) * P] for a in (HI, LO)],
                                 [xT[:, a, c, half * 512:half * 512 + 512] for a in (HI, LO)])
                                for c in range(CT)]).then_inc(dense_full, 1)

                def q_use(n):
                    g = n // 2
                    pe.wait_ge(qT_ready, i * 8 + n + 1)
                    if n == 0:
                        pe.wait_ge(bo_ready, 1)
                        pe.wait_ge(kbd_ready, i + 1)
                    for b in range(2):
                        use = 2 * n + b
                        if use >= 4:
                            pe.wait_ge(m_free, i * 16 + use - 3)
                        for k in range(2):
                            m = mm(score[:, use % 4, k * SW:(k + 1) * SW],
                                   q_e[:, n % 2, (2 * b + k) * P:(2 * b + k + 1) * P], kbd[:, g, :],
                                   start=True, stop=True)
                        m.then_inc(m_full, 1)
                    turn_tile(T("q", n), q_e[:, n % 2, :], P)

                q_proj(0)
                for n in range(1, 8):
                    q_proj(n)
                    q_use(n - 1)
                q_use(7)

                def v_proj(t):
                    d = Dn("v", t)
                    pe.wait_ge(*d.free)
                    three_pass(d.bank[:, :],
                               [([xT[:, a, c, t * P:(t + 1) * P] for a in (HI, LO)],
                                 [W["v"][:, a, c, :] for a in (HI, LO)]) for c in range(CT)]).then_inc(dense_full, 1)

                def k_proj(n, between=None):
                    g, half = n // 2, n % 2
                    if n < 2:
                        pe.wait_ge(top_struck, i * 5 + 1)
                        bank, full = score[:, n, :], k_full
                    else:
                        pe.wait_ge(*Dn("k", n).free)
                        bank, full = Dn("k", n).bank[:, :], dense_full
                    three_pass(bank,
                               [([W["k"][:, a, c, g * P:(g + 1) * P] for a in (HI, LO)],
                                 [xT[:, a, c, half * 512:half * 512 + 512] for a in (HI, LO)])
                                for c in range(CT)], between).then_inc(full, 1)

                v_proj(0)
                pe.wait_ge(m_free, i * 16 + 16)
                for t in range(LT):
                    m = nc.tensor.transpose(score[0:H, t // 4, (t % 4) * P:(t % 4 + 1) * P], mval[:, t, :], ident)
                m.then_inc(mT_full, 1)
                for t in range(1, LT):
                    v_proj(t)
                for n in range(2):
                    k_proj(n)
                pe.wait_ge(rsel_ready, i + 1)
                for p in range(NP_):
                    m = mm(score[0:HU, 2, 2 * p:2 * p + 2],
                           rsel[:, 2 * p:2 * p + 2, :].rearrange("h a u -> h (a u)"),
                           cst16[0:H, L + H * U:L + H * U + 2], start=True, stop=True)
                m.then_inc(idx_full, 1)
                k_proj(2)

                def qt_turn(p):
                    u = T("qt", p)
                    pe.wait_ge(*u.free)
                    if p < 4:
                        pe.wait_ge(qx_ready, i * 4 + p + 1)
                    else:
                        pe.wait_ge(qx_pool, i * 4 + p - 3)
                    nc.tensor.transpose(u.bank[:, 0:HU], qx[0:HU, p % 4, :], ident[0:HU, 0:HU]).then_inc(turn_full, 1)

                def qk(p):
                    g = p // 2
                    pe.wait_ge(qtT_ready, i * NP_ + p + 1)
                    pe.wait_ge(k_ready, i * 8 + 2 * g + 2)
                    if p >= 2:
                        pe.wait_ge(exp_done, i * NP_ + p - 1)
                    for h in range(2):
                        for a in (HI, LO):
                            m = mm(score[0:HU, 2 * (p % 2) + h, :], qtT[:, p % 4, a, :],
                                   kp[:, p % 4, h * 512:h * 512 + 512], start=(a == HI), stop=(a == LO))
                    m.then_inc(s_full, 1)

                def p_turn(p):
                    pe.wait_ge(prob_ready, i * NP_ + p + 1)
                    for h in range(2):
                        u = T("p", p, h)
                        pe.wait_ge(*u.free)
                        for t in range(4):
                            m = nc.tensor.transpose(u.bank[:, t * P:t * P + HU],
                                                    prob[0:HU, p % 2, (4 * h + t) * P:(4 * h + t + 1) * P],
                                                    ident[0:HU, 0:HU])
                        m.then_inc(turn_full, 1)

                def pv(p):
                    d = Dn("pv", p)
                    pe.wait_ge(*d.free)
                    pe.wait_ge(pT_ready, i * 2 * NP_ + 2 * p + 2)
                    if p == 0:
                        pe.wait_ge(v_ready, i * LT + LT)
                    for t in range(LT):
                        m = mm(d.bank[0:KR, 0:2 * DK], pT[:, p % 2, t, 0:KR], v_x1[:, t, p * 2 * DK:(p + 1) * 2 * DK],
                               start=(t == 0), stop=(t == LT - 1))
                    m.then_inc(dense_full, 1)

                def scatter(g):
                    pe.wait_ge(delta_ready, i * NP_ + 2 * g + 2)
                    pe.wait_ge(oh_ready, i * NP_ + 2 * g + 2)
                    for h in range(2):
                        d = Dn("sc", g, h)
                        pe.wait_ge(*d.free)
                        for n, (e, a) in enumerate(((0, HI), (0, LO), (1, HI), (1, LO))):
                            m = mm(d.bank[:, :], delta[0:KR, g % 2, e, a, :], oh[0:KR, 2 * (g % 2) + e, h * 512:h * 512 + 512],
                                   start=(n == 0), stop=(n == 3))
                        m.then_inc(dense_full, 1)

                def o_part(t, groups):
                    if groups[0] == 0 and t % 2 == 0:
                        pe.wait_ge(exp_done, i * NP_ + NP_ - 1 + t // 2)
                    if t == 0:
                        pe.wait_ge(ctx_ready, i * 8 + {0: 4, 2: 6, 3: 7}[groups[0]])
                    todo = [(a, b, g) for g in groups for a, b in ((HI, HI), (HI, LO), (LO, HI))]
                    for n, (a, b, g) in enumerate(todo):
                        m = mm(score[:, t, :], xT[:, a, g, t * P:(t + 1) * P], W["o"][:, b, g, :],
                               start=(g == 0 and n == 0), stop=(g == CT - 1 and n == len(todo) - 1))
                    if groups[-1] == CT - 1:
                        m.then_inc(o_full, 1)

                k_proj(3, between=lambda: qt_turn(0))
                qt_turn(1)
                qk(0)
                qt_turn(2)
                for p in range(NP_):
                    if p + 1 < NP_:
                        qk(p + 1)
                    if p + 3 < NP_:
                        qt_turn(p + 3)
                    if p < 4:
                        k_proj(4 + p)
                    if p == NP_ - 1:
                        o_part(1, (0, 1))
                    if p >= 1:
                        pv(p - 1)
                    if p in SCATTER_AT:
                        scatter(SCATTER_AT[p])
                    if p == NP_ - 2:
                        o_part(0, (0, 1))
                    p_turn(p)
                o_part(2, (0, 1)), o_part(3, (0, 1))
                pv(NP_ - 1)
                o_part(0, (2,)), o_part(1, (2,))
                scatter(3)
                o_part(2, (2,)), o_part(3, (2,))
                for t in range(4):
                    o_part(t, (3,))

                def o_proj(t):
                    d = Dn("o", t)
                    pe.wait_ge(*d.free)
                    if t == 4:
                        pe.wait_ge(ctx_ready, i * 8 + 8)
                    three_pass(d.bank[:, :],
                               [([xT[:, a, g, t * P:(t + 1) * P] for a in (HI, LO)],
                                 [W["o"][:, a, g, :] for a in (HI, LO)]) for g in range(CT)]).then_inc(dense_full, 1)

                def x2_turn(t):
                    pe.wait_ge(norm_done[1], i * LT + t + 1)
                    turn_tile(T("x2", t), xn2[:, t % 2, :], P)

                def x_turn(n):
                    pe.wait_ge(norm_done[0], i * LT + NS + LT + n + 1)
                    turn_tile(T("x", n), xn1[:, n % 2, :], P)

                def fourier(t):
                    d = Dn("f", t)
                    pe.wait_ge(*d.free)
                    if t == 0:
                        pe.wait_ge(g_lo, 4)
                    pe.wait_ge(x2T_ready, i * LT + t + 1)
                    three_pass(d.bank[:, :],
                               [([x2T[:, t % 2, a, c, :] for a in (HI, LO)],
                                 [W["g"][:, a, c, :] for a in (HI, LO)]) for c in range(CT)]).then_inc(dense_full, 1)

                o_proj(4)
                o_proj(5)
                x2_turn(0)
                o_proj(6)
                x2_turn(1)
                o_proj(7)
                for t in range(LT):
                    fourier(t)
                    if t + 2 < LT:
                        x2_turn(t + 2)
                    if not last:
                        x_turn(t)

            pe.wait_ge(weight_lo, 4)
            pe.wait_ge(ksr_ready, NS)
            with pe.Fori(0, LAST) as i:
                batch(i, False)
            batch(LAST, True)

        @block.vector
        def _(dve):
            v = nc.vector

            counted = [0, 0]

            def stats(which, n, src, rows):
                v.bn_stats(bst[0:rows, which, n, :], src).then_inc(stats_done, 1)
                counted[1] += 1
                dve.wait_ge(stats_done, counted[0] + counted[1])
                standing(dve)
                v.bn_aggr(mv[which][0:rows, n, :], bst[0:rows, which, n, :]).then_inc(mean_ready[which], 1)

            def lo_of_turn(u, hi, lo, hi_sem, hi_at, done):
                dve.wait_ge(hi_sem, hi_at)
                v.tensor_tensor(lo, u.bank[:, :].rearrange("p (c l) -> p c l", c=CT)[:, :, 0:lo.shape[-1]],
                                hi.bitcast(F32), ALU.subtract).then_inc(done, 1)

            def xT_lo(u, n, at):
                cols_ = slice(n * P, (n + 1) * P)
                lo_of_turn(u, xT[:, HI, :, cols_], xT[:, LO, :, cols_], xT_hi, at, xT_ready)

            dve.sem_inc(out_ready, 2)
            dve.wait_ge(positions_in, 32)
            r = slice(0, SR)
            v.tensor_copy(soff[r, 0], sidx[r, :]).then_inc(soff_step, 1)
            dve.wait_ge(soff_step, 1)
            v.tensor_scalar(soff[r, 1], soff[r, 0], 0.0, float(L), ALU.is_lt, ALU.mult).then_inc(soff_step, 1)
            dve.wait_ge(soff_step, 2)
            v.tensor_tensor(soff[r, 2], soff[r, 0], soff[r, 1], ALU.add).then_inc(soff_step, 1)
            dve.wait_ge(soff_step, 3)
            v.tensor_scalar(soff[r, 3], soff[r, 2], 0.0, float(L - 1), ALU.max, ALU.min).then_inc(soff_step, 1)
            dve.wait_ge(soff_step, 4)
            v.tensor_tensor(soff[r, 4], soff[r, 3], sbs[r, :], ALU.add).then_inc(soff_step, 1)
            dve.wait_ge(soff_step, 5)
            v.tensor_copy(soffu[r, :], soff[r, 4]).then_inc(soff_ready, 1)

            def first_stats(m):
                if m < NS:
                    dve.wait_ge(sampled_in[m % 4], 16 * (m // 4 + 1))
                    stats(0, m, stage[0:SR, m % 4, :], SR)
                elif m < NS + LT:
                    n = m - NS
                    wait_stage(dve, 0, 0, n)
                    if n < NS:
                        dve.wait_ge(norm_done[0], n + 1)
                    stats(0, n, stage[:, n % 4, :], P)

            def weight(n):
                w = "kqvo"[n]
                dve.wait_ge(weight_hi, n + 1)
                v.tensor_tensor(W[w][:, LO], prob[:, :, :].rearrange("p a (b n) -> p (a b) n", n=D),
                                W[w][:, HI].bitcast(F32), ALU.subtract).then_inc(weight_lo, 1)

            up, down = slice(1, FH - 1), slice(D - 1, D // 2, -1)

            def g_join(j):
                if j < 4:
                    dve.wait_ge(g_copied, 2 * j + 1)
                    v.tensor_tensor(v_x1[:, j, 0:FH], score[:, 0, 0:FH], scr[:, 0:FH], ALU.add)
                    v.tensor_tensor(v_x1[:, j, down], score[:, 0, up], scr[:, up], ALU.subtract)
                    dve.wait_ge(g_copied, 2 * j + 2)
                    v.tensor_tensor(v_x1[:, 4 + j, 0:FH], score[:, 2, 0:FH], scr[:, 258:258 + FH], ALU.subtract)
                    v.scalar_tensor_tensor(v_x1[:, 4 + j, down], score[:, 2, up], -1.0, scr[:, 259:258 + FH - 1],
                                           ALU.mult, ALU.subtract).then_inc(g_joined, 1)
                else:
                    dve.wait_ge(g_copied, 8 + j - 3)
                    bank = 2 * (j % 2)
                    if j > 4:
                        dve.wait_ge(g_lo, j - 4)
                    v.scalar_tensor_tensor(scr[:, 0:FH], score[:, bank, 0:FH], 1.0 / D, scr[:, 516:516 + FH],
                                           ALU.mult, ALU.add)
                    v.scalar_tensor_tensor(scr[:, down], score[:, bank, up], 1.0 / D, scr[:, 517:516 + FH - 1],
                                           ALU.mult, ALU.subtract).then_inc(g_joined, 1)
                    dve.wait_ge(g_hi, j - 3)
                    v.tensor_tensor(W["g"][:, LO, j - 4, :], scr[:, 0:D], W["g"][:, HI, j - 4, :].bitcast(F32),
                                    ALU.subtract).then_inc(g_lo, 1)

            def first_work(key):
                kind, k = key
                if kind == "s":
                    xs = (xs0, xs1)[k % 2]
                    lo_of_turn(first_turn(*key), xs[:, HI], xs[:, LO], xs_hi, k + 1, xs_ready)
                    first_stats(k + 4)
                elif kind == "x":
                    xT_lo(first_turn(*key), k, k + 1)
                    first_stats(NS + k + 4)

            for j in range(8):
                for key in MIDDLE[j]:
                    first_work(key)
                g_join(j)
                if j == 0:
                    first_stats(0), first_stats(1), first_stats(2), first_stats(3)
                    dve.wait_ge(bias_in, 80)
                    for c in range(CT):
                        m = v.tensor_copy(xn2[:, 0, c * P:(c + 1) * P],
                                          bv_c[:, c:c + 1].broadcast_to([P, P]))
                    m.then_inc(bv_spread, 1)
                    dve.wait_ge(consts_in, 32)
                    v.tensor_copy(idxc[:, :], cst[:, C_IDX0:C_IDX0 + NP_]).then_inc(soff_step, 1)
                if j < 2:
                    weight(j)
                if j == 3:
                    weight(2)
                if j == 6:
                    weight(3)
                for key in AFTER[j]:
                    first_work(key)
            dve.wait_ge(bo_full, 1)
            v.tensor_tensor(bo_b[:, :], score[:, 0, :], bo_b[:, :], ALU.add).then_inc(bo_ready, 1)

            def batch(i, last):
                T = lambda *k: turn_use(k, i, last)
                Dn = lambda *k: dense_use(k, i)

                counted[:] = [i * 2 * LT + NS + LT, 0]

                dve.wait_ge(ks_in, i * 16 + 16)
                for h in range(4):
                    v.tensor_scalar(kbd[:, :, h * U:(h + 1) * U], ks[:, :, 0:U], cst[:, C_HEAD + h:C_HEAD + h + 1],
                                    SCALE, ALU.mult, ALU.mult).then_inc(kbd_step, 1)
                dve.wait_ge(kbd_step, i * 5 + 4)
                v.tensor_reduce(ksum[:, :, :], kbd[:, :, 0:4 * U].rearrange("p g (h u) -> p g h u", h=4), AX_X,
                                ALU.add).then_inc(kbd_step, 1)
                dve.wait_ge(kbd_step, i * 5 + 5)
                v.tensor_scalar(kbd[:, :, 4 * U:SW], ksum[:, :, :], 1.0 / U, None, ALU.mult).then_inc(kbd_ready, 1)

                def bn1(n):
                    if last or n >= LT:
                        return
                    wait_stage(dve, i, 1, n)
                    stats(0, n, stage[:, n % 4, :], P)

                for n in range(8):
                    g, half = n // 2, n % 2
                    for b in range(2):
                        use = 2 * n + b
                        t0 = half * 4 + 2 * b
                        s = score[:, use % 4, 0:2 * SW].rearrange("p (t k) -> p t k", t=2)
                        dve.wait_ge(m_full, i * 16 + use + 1)
                        mslot = mval[:, t0:t0 + 2, 4 * g:4 * g + 4]
                        v.tensor_reduce(mslot, s[:, :, 0:4 * U].rearrange("p t (h u) -> p t h u", h=4), AX_X,
                                        ALU.max).then_inc(m_max, 1)
                        dve.wait_ge(m_max, i * 16 + use + 1)
                        v.tensor_tensor(mslot, mslot, s[:, :, 4 * U:SW], ALU.subtract).then_inc(m_free, 1)
                    if 2 <= n < 6:
                        bn1(n - 2)

                dve.wait_ge(mT_full, i + 1)
                for r in range(6):
                    r8 = slice(8 * r, 8 * r + 8)
                    src = score[0:H, 0:2, :].rearrange("h a l -> h (a l)") if r == 0 else mT[:, :]
                    if r:
                        dve.wait_ge(top_struck, i * 5 + r)
                    standing(dve)
                    v.max(top_v[:, r8], src).then_inc(top_max, 1)
                    dve.wait_ge(top_max, i * 6 + r + 1)
                    standing(dve)
                    v.max_index(top_i[:, r8], top_v[:, r8], src).then_inc(top_found, 1)
                    if r < 5:
                        v.match_replace(mT[:, :], top_v[:, r8], src, -3.0e38).then_inc(top_struck, 1)
                dve.wait_ge(top_found, i * 6 + 6)
                v.tensor_copy(top_f[:, :], top_i[:, :]).then_inc(top_float, 1)
                dve.wait_ge(top_float, i + 1)
                v.tensor_tensor(rsel[:, :, :], top_f[:, 0:U].unsqueeze(1).broadcast_to([H, H, U]),
                                cst16[0:H, L:L + H * U].rearrange("h (a u) -> h a u", a=H), ALU.mult
                                ).then_inc(rsel_ready, 1)

                def k_lo(n):
                    bank = score[:, n, :] if n < 2 else Dn("k", n).bank
                    g, half = n // 2, n % 2
                    cols_ = slice(half * 512, half * 512 + 512)
                    dve.wait_ge(k_hi, i * 8 + n + 1)
                    for e in range(2):
                        r_, to = slice(64 * e, 64 * e + 64), slice(64 - 64 * e, 128 - 64 * e)
                        slot = 2 * (g % 2) + e
                        m = v.scalar_tensor_tensor(kp[to, slot, cols_], bank[r_, :], bk_c[r_, g:g + 1],
                                                   kp[r_, slot, cols_].bitcast(F32), ALU.add, ALU.subtract)
                    m.then_inc(k_ready, 1)

                dve.wait_ge(idx_full, i + 1)
                cols = score[0:HU, 2, 0:2 * NP_].rearrange("r (p two) -> r p two", two=2)[:, :, 0]
                v.tensor_copy(idxc[0:HU, :], cols).then_inc(idxc_ready, 1)
                v.scalar_tensor_tensor(qidx[0:HU, :], cols, float(H), cst[0:HU, C_HROW:C_HROW + NP_], ALU.mult,
                                       ALU.add).then_inc(qidx_ready, 1)

                def spread_q(p):
                    dve.wait_ge(q_gathered[p], i * 16 + 16)
                    spread(v, p).then_inc(qx_ready, 1)

                def row_max(p):
                    dve.wait_ge(s_full, i * NP_ + p + 1)
                    v.tensor_reduce(negmax[0:HU, p % 2, 0:1], score[0:HU, 2 * (p % 2):2 * (p % 2) + 2, :],
                                    AX_XY, ALU.max).then_inc(s_max, 1)
                    dve.wait_ge(s_max, i * NP_ + p + 1)
                    v.tensor_scalar(negmax[0:HU, p % 2, 1:2], negmax[0:HU, p % 2, 0:1], -SCALE, None,
                                    ALU.mult).then_inc(negmax_ready, 1)

                def weights(p):
                    dve.wait_ge(exp_done, i * NP_ + p + 1)
                    v.reciprocal(psum_[0:HU, p % 2, 1:2], psum_[0:HU, p % 2, 0:1]).then_inc(recip_done, 1)
                    dve.wait_ge(recip_done, i * NP_ + p + 1)
                    v.tensor_scalar(prob[0:HU, p % 2, :], prob[0:HU, p % 2, :], psum_[0:HU, p % 2, 1:2], -1.0 / L,
                                    ALU.mult, ALU.add).then_inc(prob_ready, 1)

                def delta_of(p):
                    g, e = p // 2, p % 2
                    d = Dn("pv", p)
                    cols_ = slice(e * 2 * DK, (e + 1) * 2 * DK)
                    dve.wait_ge(dense_full, d.full_at)
                    v.tensor_tensor(dtmp[0:KR, e, :], d.bank[0:KR, 0:2 * DK], cst[0:KR, C_DMASK:C_DMASK + 2 * DK],
                                    ALU.mult).then_inc(dtmp_ready, 1)
                    dve.wait_ge(dtmp_ready, i * NP_ + p + 1)
                    v.tensor_copy(delta[0:KR, g % 2, e, HI, cols_], dtmp[0:KR, e, :]).then_inc(delta_hi, 1)
                    dve.wait_ge(delta_hi, i * NP_ + p + 1)
                    v.tensor_tensor(delta[0:KR, g % 2, e, LO, cols_], dtmp[0:KR, e, :],
                                    delta[0:KR, g % 2, e, HI, cols_].bitcast(F32), ALU.subtract).then_inc(delta_ready, 1)

                def ctx_lo(g):
                    for h in range(2):
                        d = Dn("sc", g, h)
                        cols_ = slice(h * 512, h * 512 + 512)
                        dve.wait_ge(ctx_hi, i * 8 + 2 * g + h + 1)
                        v.tensor_tensor(xT[:, LO, g, cols_], d.bank[:, :], xT[:, HI, g, cols_].bitcast(F32),
                                        ALU.subtract).then_inc(ctx_ready, 1)

                def qt_lo(p):
                    u = T("qt", p)
                    dve.wait_ge(qtT_hi, i * NP_ + p + 1)
                    v.tensor_tensor(qtT[:, p % 4, LO, :], u.bank[:, 0:HU], qtT[:, p % 4, HI, :].bitcast(F32),
                                    ALU.subtract).then_inc(qtT_ready, 1)

                k_lo(0), k_lo(1)
                spread_q(0), spread_q(1)
                qt_lo(0)
                k_lo(2)
                qt_lo(1), spread_q(2), spread_q(3)
                row_max(0), qt_lo(2), k_lo(3), qt_lo(3), weights(0), row_max(1)
                for p in range(1, NP_):
                    if p + 1 < NP_:
                        row_max(p + 1)
                    if p == 1:
                        k_lo(4)
                    if p + 3 < NP_:
                        qt_lo(p + 3)
                    if p >= 4:
                        delta_of(p - 1)
                    elif p >= 2:
                        delta_of(p - 2)
                    weights(p)
                    if p < 4:
                        k_lo(4 + p)
                    if p == 3:
                        delta_of(2)
                    if p in SCATTER_AT:
                        ctx_lo(SCATTER_AT[p])
                delta_of(NP_ - 1)
                ctx_lo(3)

                def res1(t):
                    if t < 4:
                        bank = score[:, t, :]
                        dve.wait_ge(o_full, i * 4 + t + 1)
                    else:
                        bank = Dn("o", t).bank[:, :]
                        dve.wait_ge(dense_full, Dn("o", t).full_at)
                    dve.wait_ge(bo_added, i * LT + t + 1)
                    v.tensor_tensor(v_x1[:, t, :], bank, v_x1[:, t, :], ALU.add).then_inc(x1_ready, 1)

                def bn2(t):
                    dve.wait_ge(x1_ready, i * LT + t + 1)
                    stats(1, t, v_x1[:, t, :], P)

                def x2_lo(t):
                    u = T("x2", t)
                    dve.wait_ge(x2T_hi, i * LT + t + 1)
                    v.tensor_tensor(x2T[:, t % 2, LO, :, :], u.bank[:, :].rearrange("p (c l) -> p c l", c=CT),
                                    x2T[:, t % 2, HI, :, :].bitcast(F32), ALU.subtract).then_inc(x2T_ready, 1)

                def fin_out(t):
                    d = Dn("f", t)
                    dve.wait_ge(dense_full, d.full_at)
                    dve.wait_ge(fb_added, i * LT + t + 1)
                    v.tensor_tensor(v_x1[:, t, :], d.bank[:, :], v_x1[:, t, :], ALU.add).then_inc(out_ready, 1)

                for t in range(6):
                    res1(t)
                    if t == 4:
                        bn2(3)
                    if t != 3:
                        bn2(t)
                x2_lo(0), res1(6), bn2(6), x2_lo(1), res1(7), bn2(7)
                for t in range(LT):
                    fin_out(t)
                    if t + 2 < LT:
                        x2_lo(t + 2)
                    if not last:
                        xT_lo(T("x", t), t, i * LT + LT + t + 1)
                    bn1(t + 4)

            dve.wait_ge(cleared, 4)
            with dve.Fori(0, LAST) as i:
                batch(i, False)
            batch(LAST, True)


_INS = ["x", "wq", "bq", "wk", "bk", "wv", "bv", "wo", "bo", "wfr", "wfi", "fbias", "c32", "c16", "trig", "sbase", "spos"]


def kernel(L0_attn_x, L0_attn_Wq, L0_attn_bq, L0_attn_Wk, L0_attn_bk, L0_attn_Wv, L0_attn_bv, L0_attn_Wo,
           L0_attn_bo, L0_attn_idx_k, L0_ffn_w_freq_real, L0_ffn_w_freq_imag, L0_ffn_bias):
    import concourse.bacc as bacc
    from concourse.bass_utils import run_bass_kernel_spmd

    x = np.ascontiguousarray(L0_attn_x)
    idx_k = np.ascontiguousarray(L0_attn_idx_k)
    c32, c16, trig, sbase = constants(*shapes_of(x, idx_k))
    turned = [np.ascontiguousarray(np.asarray(w).T) for w in (L0_attn_Wq, L0_attn_Wk, L0_attn_Wv, L0_attn_Wo)]
    bq, bk, bv = [column_tiles(b) for b in (L0_attn_bq, L0_attn_bk, L0_attn_bv)]
    values = [x, turned[0], bq, turned[1], bk, turned[2], bv, turned[3], L0_attn_bo,
              L0_ffn_w_freq_real, L0_ffn_w_freq_imag, L0_ffn_bias, c32, c16, trig, sbase,
              sample_positions(idx_k, x.shape[0])]
    nc = bacc.Bacc("TRN2", target_bir_lowering=False, num_devices=1, dynamic_dma_scratch_size=8192)
    arrays, args = {}, []
    for name, a in zip(_INS, values):
        a = np.ascontiguousarray(a)
        arrays[f"in_{name}"] = a
        args.append(nc.dram_tensor(f"in_{name}", a.shape, mybir.dt.from_np(a.dtype), kind="ExternalInput").ap())
    out = nc.dram_tensor("out", x.shape, F32, kind="ExternalOutput").ap()
    build(nc, *args, out)
    r = run_bass_kernel_spmd(nc, [arrays], core_ids=[0])
    return r.results[0]["out"]
```
